# Optimizing a Trainium2 kernel written in Bass

```python
import numpy as np
import jax
import jax.numpy as jnp

def _softmax(x, axis=-1):
    return jax.nn.softmax(x, axis=axis)
def _gelu(x):
    return jax.nn.gelu(x, approximate=True)
def _silu(x):
    return jax.nn.silu(x)
def _sigmoid(x):
    return jax.nn.sigmoid(x)
def _layernorm(x, axis=-1, eps=1e-5):
    m = jnp.mean(x, axis=axis, keepdims=True)
    v = jnp.var(x, axis=axis, keepdims=True)
    return (x - m) / jnp.sqrt(v + eps)
def _scatter_add(tgt, idx, src, axis=0):
    return tgt.at[idx].add(src)
def _segment_sum(src, seg, n):
    return jax.ops.segment_sum(src, seg, n)

kernel_name = 'mk_adj_preln_d2_adj_256_b3ee7e'

def setup_inputs(seed: int = 0):
    np.random.seed(seed)
    _w = jnp.asarray
    def _rec_inputs():
        import jax
        import jax.numpy as jnp
        _gk = jax.random.key(seed)
        x = -0.0005146 + 1 * jax.random.normal(jax.random.fold_in(_gk, 1), (8, 2048, 256), jnp.float32)
        _a = jax.random.bernoulli(jax.random.fold_in(_gk, 2), 0.015625, (8, 2048, 2048))
        _a = jnp.logical_or(_a, jnp.swapaxes(_a, -1, -2))
        _a = jnp.logical_or(_a, jnp.eye(2048, dtype=bool))
        adj = _a.astype(jnp.int32)
        return x, adj
    x, adj = _rec_inputs()
    def _L0_gnn_setup():
        import jax, jax.numpy as jnp
        import numpy as np
        B, N, C, OUT, S = (4, 2048, 256, 256, 25)
        DENSITY = 0.008
        key = jax.random.key(seed)
        kA, kX, kW = jax.random.split(key, 3)
        A = jax.random.bernoulli(kA, DENSITY, (B, N, N)).astype(jnp.int32)
        X = jax.random.normal(kX, (B, N, C), dtype=jnp.float32)
        W = jax.random.normal(kW, (2 * C, OUT), dtype=jnp.float32) * np.float32(1.0 / np.sqrt(2 * C))
        b = jnp.zeros((OUT,), dtype=jnp.float32)
        return {'A': A, 'X': X, 'W': W, 'b': b}
    _L0_gnn_all = _L0_gnn_setup()
    _L0_gnn_in = {k: v for k, v in _L0_gnn_all.items() if k in ('W', 'b', )}
    del _L0_gnn_all

    def _L1_gnn_setup():
        import jax, jax.numpy as jnp
        import numpy as np
        B, N, F_IN, F_OUT = (8, 2048, 256, 256)
        key = jax.random.key(seed)
        k1, k2, k3, k4 = jax.random.split(key, 4)
        inp = jax.random.normal(k1, (B, N, F_IN), dtype=jnp.float32)
        adj = jax.random.randint(k2, (B, N, N), 0, 2, dtype=jnp.int32)
        W = jax.random.normal(k3, (F_IN, F_OUT), dtype=jnp.float32) * (1.414 * (6.0 / (F_IN + F_OUT)) ** 0.5)
        a = jax.random.normal(k4, (2 * F_OUT, 1), dtype=jnp.float32) * (1.414 * (6.0 / (2 * F_OUT + 1)) ** 0.5)
        return {'inp': inp, 'adj': adj, 'W': W, 'a': a}
    _L1_gnn_all = _L1_gnn_setup()
    _L1_gnn_in = {k: v for k, v in _L1_gnn_all.items() if k in ('W', 'a', )}
    del _L1_gnn_all

    return {
        "x": x,
        "adj": adj,
        "L0_gnn_W": _L0_gnn_in["W"],
        "L0_gnn_b": _L0_gnn_in["b"],
        "L1_gnn_W": _L1_gnn_in["W"],
        "L1_gnn_a": _L1_gnn_in["a"],
    }

def reference(x, adj, L0_gnn_W, L0_gnn_b, L1_gnn_W, L1_gnn_a):
    import jax
    import jax.numpy as jnp
    def _L0_gnn_ref(A, X, W, b):
        import jax, jax.numpy as jnp
        import numpy as np
        B, N, C, OUT, S = (4, 2048, 256, 256, 25)
        DENSITY = 0.008
        mask = A != 0
        neg_inf = jnp.float32(-jnp.inf)
        pri = -jnp.arange(N, dtype=jnp.float32)
        scores = jnp.where(mask, pri, neg_inf)
        vals, idx = jax.lax.top_k(scores, S)
        valid = vals > neg_inf
        feats = jax.vmap(lambda x, i: x[i])(X, idx)
        feats = jnp.where(valid[..., None], feats, neg_inf)
        agg = feats.max(axis=2)
        degree = mask.sum(axis=-1)
        agg = jnp.where((degree <= S)[..., None], jnp.maximum(agg, 0.0), agg)
        h = jnp.concatenate([X, agg], axis=-1)
        out = jax.nn.relu(jnp.einsum('bnf,fo->bno', h, W) + b)
        return out

    def _L1_gnn_ref(inp, adj, W, a):
        import jax, jax.numpy as jnp
        import numpy as np
        B, N, F_IN, F_OUT = (8, 2048, 256, 256)
        h = jnp.einsum('bnf,fo->bno', inp, W)
        a1 = a[:F_OUT, 0]
        a2 = a[F_OUT:, 0]
        s1 = h @ a1
        s2 = h @ a2
        e = jax.nn.leaky_relu(s1[:, :, None] + s2[:, None, :], negative_slope=0.4)
        att = jnp.where(adj > 0, e, jnp.float32(-1e+20))
        att = jax.nn.softmax(att, axis=1)
        h_prime = jnp.einsum('bij,bjo->bio', att, h)
        return jax.nn.gelu(h_prime, approximate=False)

    h = jnp.maximum(_layernorm(x, axis=-1), 0.0)
    x = x + _L0_gnn_ref(adj, h, L0_gnn_W, L0_gnn_b)
    h = jnp.maximum(_layernorm(x, axis=-1), 0.0)
    x = x + _L1_gnn_ref(h, adj, L1_gnn_W, L1_gnn_a)
    return x


_drawn_inputs = setup_inputs


def setup_inputs(seed=0):
    import zlib

    import numpy as np

    out = dict(_drawn_inputs(seed))
    spreads = {'L0_gnn_b': (0.0, 0.1)}
    factors = {}
    for name, (base, spread) in spreads.items():
        noise = np.random.default_rng([zlib.crc32(name.encode()), seed]).standard_normal(out[name].shape)
        drawn = base * np.exp(spread * noise) if base else spread * noise
        out[name] = jnp.asarray(drawn.astype(out[name].dtype))
    for name, factor in factors.items():
        out[name] = (out[name] * factor).astype(out[name].dtype)
    return out
```

```python
from contextlib import ExitStack

import concourse.bass as bass
from concourse import mybir

fp32 = mybir.dt.float32
bf16 = mybir.dt.bfloat16
i32 = mybir.dt.int32
u8 = mybir.dt.uint8
ALU = mybir.AluOpType
ACT = mybir.ActivationFunctionType
AX = mybir.AxisListType

P = 128
NB, N, C = 8, 2048, 256
TILES = N // P
HALF = N // 2
KEEP = 25
ROWS = N + 1
WORD = 8
WORDS = N // WORD
CHUNKS = (9, 8, 8)
PAIRS = TILES // 2
EPS = 1e-5
SLOPE = 0.4
BLOCKED = 1e30

C_ID, C_PACK, C_KEY, C_IOTA = 0, P, P + 16, P + 16 + WORDS
C_COLS = C_IOTA + WORD


class Order:

    def __init__(self, sem):
        self.sem, self.n = sem, 0

    def mark(self, instruction):
        instruction.then_inc(self.sem, 1)
        self.n += 1
        return self.n


def graph_layers(nc, x, adj, W0, b0, W1, a1, const_f, const_i, out):
    ctx = ExitStack()
    with ctx:
        def sb(name, shape, dt):
            return ctx.enter_context(nc.sbuf_tensor(name, shape, dt))

        def ps(name, shape, dt):
            return ctx.enter_context(nc.psum_tensor(name, shape, dt))

        def sem(name):
            return ctx.enter_context(nc.semaphore(name))

        table = [nc.dram_tensor(f"h_table{u}", (ROWS, C), fp32).ap() for u in range(2)]
        edges_t = nc.dram_tensor("edges_t", (NB * N, N), u8).ap()
        x1_dram = nc.dram_tensor("x1_rows", (NB * N, C), fp32).ap()
        x_rows = x.rearrange("b n c -> (b n) c")
        adj_rows = adj.rearrange("b n m -> (b n) m")
        out_rows = out.rearrange("b n c -> (b n) c")

        cf = sb("cf", [P, C_COLS], fp32)
        cb = sb("cb", [P, P + 16], bf16)
        ci = sb("ci", [P, WORD], i32)
        ident, identb, pack = cf[:, C_ID:C_ID + P], cb[:, 0:P], cb[:, P:P + 16]
        w0 = sb("w0", [P, 4, C], fp32)
        w1 = sb("w1", [P, 2, C + 1], fp32)
        wa1 = sb("wa1", [P, 2, P], fp32)
        bias0 = sb("bias0", [1, C], fp32)
        ones = sb("ones", [1, P], fp32)
        zeros = sb("zeros", [1, 512], bf16)
        zrow = sb("zrow", [1, C], fp32)

        xn = [sb(f"xn{u}", [P, 2, C], fp32) for u in range(2)]
        hn = [sb(f"hn{u}", [P, 2, C], fp32) for u in range(2)]
        bn6 = sb("bn6", [P, 3, 6], fp32)
        mv = [sb(f"mv{u}", [P, 3, 2], fp32) for u in range(2)]
        std = [sb(f"std{u}", [P, 3], fp32) for u in range(2)]
        rs = [sb(f"rs{u}", [P, 3], fp32) for u in range(2)]
        nmr = [sb(f"nmr{u}", [P, 3], fp32) for u in range(2)]
        lt = sb("lt", [P, 2, 3], fp32)
        ad = [sb(f"ad{u}", [P, N], i32) for u in range(2)]
        sg = sb("sg", [P, N], bf16)
        bits = sg[:, :].rearrange("p (m n) -> p m n", n=P)
        stage = sb("stage", [P, TILES, 8 * P], u8)
        wv = sb("wv", [P, WORDS], fp32)
        wt = sb("wt", [P, WORDS], fp32)
        top = sb("top", [P, 32], fp32)
        topi = sb("topi", [P, KEEP], i32)
        hi = sb("hi", [P, KEEP], i32)
        bt = sb("bt", [P, KEEP, WORD], i32)
        cand = sb("cand", [P, KEEP, WORD], fp32)
        cand2 = sb("cand2", [P, KEEP, WORD], fp32)
        top2 = sb("top2", [P, 32], fp32)
        idx = [sb(f"idx{u}", [P, KEEP], i32) for u in range(2)]
        gb = [sb(f"gb{c}", [P, n + (c > 0), C], fp32) for c, n in enumerate(CHUNKS)]
        xl = [sb(f"xl{u}", [P, C], fp32) for u in range(2)]
        hl = [sb(f"hl{u}", [P, 2, C], fp32) for u in range(2)]
        hcat = sb("hcat", [P, 4, P], fp32)
        x1 = [sb(f"x1_{u}", [P, C], fp32) for u in range(2)]
        y1 = sb("y1", [P, C], fp32)
        h1t = sb("h1t", [P, 2, P], fp32)
        h_acc = sb("h_acc", [P, TILES, C + 1], fp32)
        s1_acc = sb("s1_acc", [P, N], fp32)
        h_all = sb("h_all", [P, TILES, C + 1], fp32)
        s1_all = sb("s1_all", [P, N], fp32)
        s2p = sb("s2p", [P, TILES], fp32)
        s2n = sb("s2n", [P, TILES], fp32)
        edge = [sb(f"edge{u}", [P, 2, N], u8) for u in range(2)]
        nbt = sb("nbt", [P, N], bf16)
        val = sb("val", [P, N], fp32)
        lk = sb("lk", [P, N], fp32)
        ex = [sb(f"ex{u}", [P, HALF], fp32) for u in range(2)]
        hz = [sb(f"hz{u}", [P, C], fp32) for u in range(2)]
        m_t = sb("m_t", [P, 3], fp32)
        nb = sb("nb", [P, TILES], fp32)
        za = [sb(f"za{u}", [P, 2], fp32) for u in range(2)]
        zs = sb("zs", [P, 1], fp32)
        rz = sb("rz", [P, TILES], fp32)
        xo = sb("xo", [P, 8, C], fp32)
        go = sb("go", [P, 8, C], fp32)

        ps_av = ps("ps_av", [P, 8 * C], fp32)
        ps_c = ps("ps_c", [P, 1024], fp32)
        ps_t = ps("ps_t", [P, 512], fp32)
        ps_l = ps("ps_l", [P, 512], fp32)
        sgt = ps_c[:, :].bitcast(bf16)
        words = ps_c[:, 0:WORDS]

        S = {n: sem(n) for n in (
            "consts_in", "weights_ready", "ones_ready", "zrow_stored",
            "signed", "signs_transposed", "bits_ready", "edges_ready", "edges_stored", "words_done", "words_read",
            "idx_ready", "stats_ready", "std_ready", "norm_ready", "hn_ready",
            "agg_ready", "cat_transposed", "cat_ready", "out0_done", "y1_ready", "y1_transposed", "h1t_ready",
            "h_done", "h_saved", "h_copied", "s1_copied",
            "blocked_ready", "val_ready", "relu_ready", "leaky_ready", "exp_ready", "hz_ready", "av_done",
            "sweep_done", "gelu_done", "xo_in", "res_ready", "out_stored", "order",
            "sp_passed", "pool_passed", "dve_passed")}
        adj_in = [sem(f"adj_in{u}") for u in range(2)]
        xn_in = [sem(f"xn_in{u}") for u in range(2)]
        hn_stored = [sem(f"hn_stored{u}") for u in range(2)]
        l_in = [sem(f"l_in{u}") for u in range(2)]
        x1_stored = [sem(f"x1_stored{u}") for u in range(2)]
        edge_in = [sem(f"edge_in{u}") for u in range(2)]
        gathered = [sem(f"gathered{c}") for c in range(3)]
        maxed = [sem(f"maxed{c}") for c in range(3)]

        def wait_apart(engine, name, semaphore, value):
            engine.wait_ge(semaphore, value)
            engine.sem_inc(S[name], 1)

        block = ctx.enter_context(nc.Block())

        @block.sync
        def _(sp):
            def load_adj(a, u):
                sp.dma_start(ad[u][:, :], adj_rows[bass.ds(a * P, P), :]).then_inc(adj_in[u], 16)

            def load_xn(m, u):
                sp.dma_start(xn[u][:, :, :], x_rows[bass.ds(m * 2 * P, 2 * P), :].rearrange("(k p) c -> p k c", p=P)
                             ).then_inc(xn_in[u], 16)

            def store_hn(tb, k, m, u):
                wait_apart(sp, "sp_passed", S["hn_ready"], m + 1)
                sp.dma_start(table[tb][k * 2 * P:(k + 1) * 2 * P, :].rearrange("(k p) c -> p k c", p=P),
                             hn[u][:, :, :]).then_inc(hn_stored[u], 16)

            def load_l(tb, b, t, u):
                sp.dma_start(xl[u][:, :], x_rows[bass.ds(b * N + t * P, P), :]).then_inc(l_in[u], 16)
                sp.dma_start(hl[u][:, 0, :], table[tb][t * P:(t + 1) * P, :]).then_inc(l_in[u], 16)

            def load_edge(bt_, t, u):
                sp.dma_start(edge[u][:, :, :], edges_t[bass.ds(bt_ * N + (t % 8) * 2 * P, 2 * P), :]
                             .rearrange("(k p) n -> p k n", p=P)).then_inc(edge_in[u], 16)

            sp.dma_start(cf[:, :], const_f).then_inc(S["consts_in"], 16)
            load_xn(0, 0)
            load_xn(1, 1)
            load_adj(0, 0)
            sp.dma_start(ci[:, :], const_i).then_inc(S["consts_in"], 16)
            sp.dma_start(w0[:, :, :], W0.rearrange("(k p) o -> p k o", p=P)).then_inc(S["consts_in"], 16)
            sp.dma_start(w1[:, :, 0:C], W1.rearrange("(k p) o -> p k o", p=P)).then_inc(S["consts_in"], 16)
            sp.dma_start(bias0[:, :], b0.rearrange("(a o) -> a o", a=1)).then_inc(S["consts_in"], 16)
            sp.dma_start(val[:, 0:2 * C], a1.rearrange("f a -> a f").partition_broadcast(P)
                         if False else a1.rearrange("f a -> a f").to_broadcast([P, 2 * C])).then_inc(S["consts_in"], 16)
            sp.sem_inc(S["edges_stored"], 16)
            for m in range(PAIRS):
                if m + 2 < PAIRS:
                    wait_apart(sp, "sp_passed", S["hn_ready"], m + 1)
                    load_xn(m + 2, m % 2)
                if m == 2:
                    load_adj(1, 1)
                store_hn(0, m, m, m % 2)
            wait_apart(sp, "sp_passed", S["ones_ready"], 1)
            for tb in range(2):
                sp.dma_start(table[tb][N:ROWS, :], zrow[:, :]).then_inc(S["zrow_stored"], 16)
            for u in range(2):
                wait_apart(sp, "sp_passed", S["signed"], u + 1)
                load_adj(2 + u, u)
            for u in range(2):
                wait_apart(sp, "sp_passed", hn_stored[u], 16 * PAIRS // 2)
            load_l(0, 0, 0, 0)

            def step(b, tb, t, n, a, l, e, w):
                v = b * TILES + t
                u = t % 2
                if n:
                    m = (b + 1) * PAIRS + t
                    wait_apart(sp, "sp_passed", S["hn_ready"], m - 1)
                    load_xn(m, u)
                if e:
                    nt = (t + 1) % 16
                    eb = b - 1 + (t + 1) // 16
                    if t == 15:
                        wait_apart(sp, "sp_passed", S["edges_stored"], 16 * 4 * eb + 16 * 5)
                    if w:
                        wait_apart(sp, "sp_passed", S["blocked_ready"], (b - 1) * 32 + 2 * t)
                    load_edge(eb, nt, nt % 2)
                if l and not (type(b) is int and b == NB - 1 and t == 15):
                    wait_apart(sp, "sp_passed", S["cat_transposed"], v)
                    wait_apart(sp, "sp_passed", S["stats_ready"], PAIRS + v)
                    if t == 15:
                        for k in range(2):
                            wait_apart(sp, "sp_passed", hn_stored[k], b * 64 + 128)
                        load_l(1 - tb, b + 1, 0, 0)
                    else:
                        load_l(tb, b, t + 1, (t + 1) % 2)
                if a:
                    wait_apart(sp, "sp_passed", S["signed"], v + 3)
                    load_adj(v + 4, u)
                if l:
                    wait_apart(sp, "sp_passed", S["stats_ready"], PAIRS + v + 1)
                    sp.dma_start(x1_dram[bass.ds(v * P, P), :], x1[u][:, :]).then_inc(x1_stored[u], 16)
                if n:
                    if t == 0:
                        wait_apart(sp, "sp_passed", maxed[2], b * TILES + 1)
                        wait_apart(sp, "sp_passed", S["cat_transposed"], b * TILES)
                    store_hn(1 - tb, t, m, u)
                if t % 4 == 1 and not (type(b) is int and b == NB - 1 and t > 13) and l:
                    g4 = b * 4 + t // 4
                    wait_apart(sp, "sp_passed", S["edges_ready"], v + 3)
                    wait_apart(sp, "sp_passed", S["edges_stored"], g4 * 16 + 16)
                    at = 4 * P * ((t // 4) % 2)
                    sp.dma_start(edges_t.rearrange("(b m p) n -> b p m n", p=P, m=TILES)[bass.ds(b, 1)]
                                 .rearrange("b p m n -> p (b m) n")[:, :, (t // 4) * 4 * P:(t // 4 + 1) * 4 * P],
                                 stage[:, :, at:at + 4 * P]).then_inc(S["edges_stored"], 16)

            def load_xo(bt_, h, f):
                wait_apart(sp, "sp_passed", S["res_ready"], f)
                for u in range(2):
                    wait_apart(sp, "sp_passed", x1_stored[u], bt_ * 128 + 128)
                sp.dma_start(xo[:, :, :], x1_dram[bass.ds(bt_ * N + h * HALF, HALF), :]
                             .rearrange("(k p) c -> p k c", p=P)).then_inc(S["xo_in"], 16)

            def store_out(bt_, h, f):
                wait_apart(sp, "sp_passed", S["res_ready"], f + 1)
                sp.dma_start(out_rows[bass.ds(bt_ * N + h * HALF, HALF), :].rearrange("(k p) c -> p k c", p=P),
                             go[:, :, :]).then_inc(S["out_stored"], 16)

            def round_(b, tb, first=False, last=False, drain=False):
                for t in range(TILES):
                    step(b, tb, t, n=t < 8 and not last and not drain, a=not drain and not (last and t >= 12),
                         l=not drain, e=(not first or t == 15) and not (drain and t == 15), w=not first)
                    if not first:
                        if t == 3:
                            if not (type(b) is int and b == 1):
                                store_out(b - 2, 1, b * 2 - 3)
                            load_xo(b - 1, 0, b * 2 - 2)
                        if t == 11:
                            store_out(b - 1, 0, b * 2 - 2)
                            load_xo(b - 1, 1, b * 2 - 1)

            round_(0, 0, first=True)
            round_(1, 1)
            with sp.Fori(2, NB - 2, 2) as b:
                round_(b, 0)
                round_(b + 1, 1)
            round_(NB - 2, 0)
            round_(NB - 1, 1, last=True)
            round_(NB, 0, drain=True)
            store_out(NB - 1, 1, 2 * NB - 1)
            wait_apart(sp, "sp_passed", S["out_stored"], 16 * 2 * NB)

        @block.gpsimd
        def _(pool):
            nc.gpsimd.memset(zeros[:, :], 0.0).then_inc(S["ones_ready"], 2)
            pool.wait_ge(S["zrow_stored"], 32)
            with pool.Fori(0, NB, 2) as b2:
                for tb in range(2):
                    b = b2 + tb
                    for u in range(2):
                        wait_apart(pool, "pool_passed", hn_stored[u], b * 64 + 64)
                    with pool.Fori(0, PAIRS) as i:
                        for u in range(2):
                            g = b * TILES + i * 2 + u
                            wait_apart(pool, "pool_passed", S["idx_ready"], g + 1)
                            k = 0
                            for c, n in enumerate(CHUNKS):
                                wait_apart(pool, "pool_passed", maxed[c], g + 1)
                                for s in range(n):
                                    pool.indirect_dma_start(gb[c][:, s + (c > 0), :], None, table[tb],
                                                            bass.IndirectOffsetOnAxis(idx[u][:, k:k + 1], 0)
                                                            ).then_inc(gathered[c], 16)
                                    k += 1

        @block.scalar
        def _(act):

            def sign(k, a, u):
                act.wait_ge(adj_in[u], k * 16 + 16)
                act.wait_ge(S["words_done"], a)
                nc.scalar.activation(sg[:, :], ad[u][:, :], ACT.Sign).then_inc(S["signed"], 1)

            def evacuate_signs(a, col):
                act.wait_ge(S["signs_transposed"], a + 1)
                nc.scalar.activation(bits, sgt.rearrange("p (m n) -> p m n", n=P), ACT.Square).then_inc(S["bits_ready"], 1)
                act.wait_ge(S["edges_stored"], a // 4 * 16)
                nc.scalar.activation(stage[:, :, bass.ds(col, P)], sgt.rearrange("p (m n) -> p m n", n=P), ACT.Relu
                                     ).then_inc(S["edges_ready"], 1)

            def root(q, u, cols):
                act.wait_ge(S["stats_ready"], q + 1)
                nc.scalar.activation(std[u][:, cols], mv[u][:, cols, 1], ACT.Sqrt, bias=EPS).then_inc(S["std_ready"], 1)

            def norm_pair(q, m, u):
                act.wait_ge(S["norm_ready"], q + 1)
                for k in range(2):
                    ins = nc.scalar.activation(hn[u][:, k, :], xn[u][:, k, :], ACT.Relu,
                                               bias=nmr[u][:, k:k + 1], scale=rs[u][:, k:k + 1])
                ins.then_inc(S["hn_ready"], 1)

            act.wait_ge(S["consts_in"], 16 * 6)
            for m in range(PAIRS):
                u = m % 2
                act.wait_ge(xn_in[u], 16 * (m // 2 + 1))
                root(m, u, slice(0, 2))
                if m >= 2:
                    act.wait_ge(hn_stored[u], 16 * (m // 2))
                norm_pair(m, m, u)
                if m == 1:
                    sign(0, 0, 0)
                if m == 3:
                    evacuate_signs(0, 0)
                if m == 5:
                    sign(0, 1, 1)
            evacuate_signs(1, P)

            def blocked(i, k, u, jj, cols):
                act.wait_ge(edge_in[u], k * 16 + 16)
                nc.scalar.activation(nbt[:, cols], edge[u][:, jj, cols], ACT.Identity, scale=BLOCKED, bias=-BLOCKED
                                     ).then_inc(S["blocked_ready"], 1)

            def relu_part(i, j, w):
                act.wait_ge(S["val_ready"], i + 1)
                act.wait_ge(S["exp_ready"], i)
                nc.scalar.activation(lk[:, 0:w], val[:, 0:w], ACT.Relu, scale=1 - SLOPE, bias=s2p[:, bass.ds(j, 1)]
                                     ).then_inc(S["relu_ready"], 1)

            def exp_part(i, j, jj, sweep):
                act.wait_ge(S["leaky_ready"], i + 1)
                act.wait_ge(S["av_done"], i)
                bias = nb[:, bass.ds(j, 1)]
                if sweep == 0:
                    nc.scalar.activation(ex[jj][:, :], lk[:, 0:HALF], ACT.Exp, bias=bias, accum_out=za[jj][:, 0:1])
                    nc.scalar.activation(lk[:, HALF:N], lk[:, HALF:N], ACT.Exp, bias=bias, accum_out=za[jj][:, 1:2]
                                         ).then_inc(S["exp_ready"], 1)
                else:
                    nc.scalar.activation(ex[jj][:, :], lk[:, 0:HALF], ACT.Exp, bias=bias).then_inc(S["exp_ready"], 1)

            def flush(f):
                act.wait_ge(S["sweep_done"], f + 1)
                act.wait_ge(S["out_stored"], f * 16)
                nc.scalar.activation(go[:, :, :], ps_av[:, :].rearrange("p (k c) -> p k c", c=C), ACT.Gelu
                                     ).then_inc(S["gelu_done"], 1)

            def step(b, i, u, sweep, n, a, l, att, fl=None):
                v = b * TILES + i * 2 + u
                k = b * PAIRS + i
                it = (b - 1) * 32 + i * 4 + u * 2
                j = i * 4 + u * 2 - 16 * sweep
                w = N if sweep == 0 else HALF
                cols = slice(0, N) if sweep == 0 else slice(HALF, N)
                if a:
                    sign(k + 1, v + 2, u)
                if att:
                    blocked(it, k - PAIRS, u, 0, cols)
                if l:
                    act.wait_ge(S["cat_transposed"], v + 1)
                    nc.scalar.copy(hcat[:, :, :], ps_t[:, :].rearrange("p (k n) -> p k n", n=P)).then_inc(S["cat_ready"], 1)
                if att:
                    relu_part(it, j, w)
                    blocked(it + 1, k - PAIRS, u, 1, cols)
                if a:
                    evacuate_signs(v + 2, (v + 2) % 8 * P)
                if l:
                    root(PAIRS + v, u, slice(0 if n else 2, 3))
                if fl is not None:
                    flush(fl)
                if att:
                    exp_part(it, j, 0, sweep)
                    relu_part(it + 1, j + 1, w)
                if l:
                    act.wait_ge(S["y1_transposed"], v + 1)
                    nc.scalar.activation(h1t[:, :, :], ps_t[:, 0:C].rearrange("p (k n) -> p k n", n=P), ACT.Relu
                                         ).then_inc(S["h1t_ready"], 1)
                if n:
                    m = (b + 1) * PAIRS + i * 2 + u
                    act.wait_ge(hn_stored[u], b * 64 + i * 16 + 64)
                    norm_pair(PAIRS + v, m, u)
                if l:
                    act.wait_ge(S["h_done"], v + 1)
                    if not (type(b) is int and b == 0):
                        act.wait_ge(S["s1_copied"], b)
                    nc.scalar.copy(h_acc[:, bass.ds(i * 2 + u, 1), :].rearrange("p a c -> p (a c)"), ps_l[:, 0:C + 1])
                    nc.scalar.copy(s1_acc[:, bass.ds((i * 2 + u) * P, P)], ps_l[:, 384:384 + P]).then_inc(S["h_saved"], 1)
                if att:
                    exp_part(it + 1, j + 1, 1, sweep)

            def hand_over(b):
                act.wait_ge(S["h_saved"], b * TILES)
                act.wait_ge(S["hz_ready"], (b - 1) * 32)
                nc.scalar.copy(h_all[:, :, :], h_acc[:, :, :]).then_inc(S["h_copied"], 1)

            def round_(b, first=False, last=False, drain=False):
                if not first:
                    hand_over(b)
                for sweep in range(2):
                    def pair(i, fl=None, a=True):
                        for u in range(2):
                            step(b, i, u, sweep, n=sweep == 0 and not last and not drain, a=a and not drain,
                                 l=not drain, att=not first, fl=fl if u == 0 else None)
                    i0 = sweep * 4
                    fl = None
                    if not first and not (type(b) is int and b == 1 and sweep == 0):
                        fl = b * 2 - 3 + sweep
                    end = i0 + 4 - (last and sweep)
                    pair(i0, fl)
                    with act.Fori(i0 + 1, end) as i:
                        pair(i)
                    if last and sweep:
                        pair(i0 + 3, a=False)

            round_(0, first=True)
            round_(1)
            with act.Fori(2, NB - 1) as b:
                round_(b)
            round_(NB - 1, last=True)
            round_(NB, drain=True)
            flush(2 * NB - 1)

        @block.vector
        def _(dve):
            order = S["order"]
            V = nc.vector

            def end_order(o):
                dve.wait_ge(order, o.n)
                dve.sem_clear(order)

            def statistics(o, src, slot, u, ready=None):
                n = o.mark(V.bn_stats(bn6[:, slot, :], src))
                dve.wait_ge(order, n)
                ins = V.bn_aggr(mv[u][:, slot, :], bn6[:, slot, :])
                if ready is not None:
                    ins.then_inc(ready, 1)
                else:
                    o.mark(ins)

            def normaliser(o, q, u, cols):
                mean, var = mv[u][:, cols, 0], mv[u][:, cols, 1]
                dve.wait_ge(S["std_ready"], q + 1)
                dve.wait_ge(order, o.n)
                n = o.mark(V.reciprocal(rs[u][:, cols], std[u][:, cols]))
                dve.wait_ge(order, n)
                n = o.mark(V.tensor_tensor(lt[:, 0, cols], rs[u][:, cols], rs[u][:, cols], ALU.mult))
                dve.wait_ge(order, n)
                n = o.mark(V.scalar_tensor_tensor(out=lt[:, 1, cols], in0=var, scalar=EPS, in1=lt[:, 0, cols],
                                                  op0=ALU.add, op1=ALU.mult))
                dve.wait_ge(order, n)
                n = o.mark(V.tensor_scalar(lt[:, 0, cols], lt[:, 1, cols], -0.5, 1.5, ALU.mult, ALU.add))
                dve.wait_ge(order, n)
                n = o.mark(V.tensor_tensor(rs[u][:, cols], rs[u][:, cols], lt[:, 0, cols], ALU.mult))
                dve.wait_ge(order, n)
                V.scalar_tensor_tensor(out=nmr[u][:, cols], in0=mean, scalar=-1.0, in1=rs[u][:, cols],
                                       op0=ALU.mult, op1=ALU.mult).then_inc(S["norm_ready"], 1)

            def eights(o, src, work, dst, n):
                for r in range(4):
                    dve.wait_ge(order, n)
                    n = o.mark(V.max(dst[:, 8 * r:8 * r + 8], src if r == 0 else work))
                    if r < 3:
                        dve.wait_ge(order, n)
                        n = o.mark(V.match_replace(work, dst[:, 8 * r:8 * r + 8], src if r == 0 else work, 0.0))
                return n

            def first_words(o, a):
                dve.wait_ge(S["words_done"], a + 1)
                dve.wait_ge(order, o.n)
                n = o.mark(V.scalar_tensor_tensor(out=wt[:, :], in0=words, scalar=0.0, in1=cf[:, C_KEY:C_KEY + WORDS],
                                                  op0=ALU.is_gt, op1=ALU.mult))
                dve.wait_ge(order, n)
                V.tensor_tensor(wv[:, :], wt[:, :], words, ALU.add).then_inc(S["words_read"], 1)
                wait_apart(dve, "dve_passed", S["words_read"], a + 1)
                n = eights(o, wv[:, :], wt[:, :], top, o.n)
                dve.wait_ge(order, n)
                n = o.mark(V.tensor_copy(topi[:, :], top[:, 0:KEEP]))
                dve.wait_ge(order, n)
                o.mark(V.tensor_scalar(hi[:, :], topi[:, :], 5, 0xFFFF8, ALU.logical_shift_right, ALU.bitwise_and))
                o.mark(V.tensor_tensor(bt[:, :, :], topi[:, :].unsqueeze(2).to_broadcast([P, KEEP, WORD]),
                                       ci[:, :].unsqueeze(1).to_broadcast([P, KEEP, WORD]), ALU.bitwise_and))

            def first_nodes(o, u):
                dve.wait_ge(order, o.n)
                n = o.mark(V.tensor_tensor(cand2[:, :, :], hi[:, :].unsqueeze(2).to_broadcast([P, KEEP, WORD]),
                                           cf[:, C_IOTA:C_IOTA + WORD].unsqueeze(1).to_broadcast([P, KEEP, WORD]),
                                           ALU.subtract))
                dve.wait_ge(order, n)
                n = o.mark(V.scalar_tensor_tensor(out=cand[:, :, :], in0=bt[:, :, :], scalar=0.0, in1=cand2[:, :, :],
                                                  op0=ALU.is_gt, op1=ALU.mult))
                n = eights(o, cand[:, :, :].rearrange("p k w -> p (k w)"),
                           cand2[:, :, :].rearrange("p k w -> p (k w)"), top2, n)
                dve.wait_ge(order, n)
                V.tensor_scalar(idx[u][:, :], top2[:, 0:KEEP], -1.0, float(N), ALU.mult, ALU.add).then_inc(S["idx_ready"], 1)

            def chunk_max(o, c, g, u=0):
                dve.wait_ge(gathered[c], (g + 1) * (16 * CHUNKS[c]))
                if c > 0:
                    dve.wait_ge(maxed[c - 1], g + 2)
                dst = gb[c + 1][:, 0, :] if c < 2 else hl[u][:, 1, :]
                if c == 2:
                    dve.wait_ge(S["cat_transposed"], g)
                dve.wait_ge(order, o.n)
                V.tensor_reduce(dst, gb[c][:, :, :].rearrange("p k c -> p c k"), AX.X, ALU.max).then_inc(maxed[c], 1)

            o = Order(order)
            V.memset(zrow[:, :], 0.0)
            V.memset(ones[:, :], 1.0).then_inc(S["ones_ready"], 1)
            for c in range(3):
                dve.sem_inc(maxed[c], 1)
            dve.wait_ge(S["consts_in"], 16 * 6)
            o.mark(V.tensor_copy(cb[:, :], cf[:, 0:P + 16]))
            for k in range(2):
                n = o.mark(V.tensor_tensor(lk[:, 0:2 * C].rearrange("p (a o) -> p a o", a=2),
                                           w1[:, k, 0:C].unsqueeze(1).to_broadcast([P, 2, C]),
                                           val[:, 0:2 * C].rearrange("p (a o) -> p a o", a=2), ALU.mult))
                dve.wait_ge(order, n)
                n = o.mark(V.tensor_reduce(m_t[:, 0:2], lk[:, 0:2 * C].rearrange("p (a o) -> p a o", a=2), AX.X, ALU.add))
                dve.wait_ge(order, n)
                o.mark(V.tensor_copy(w1[:, k, C:C + 1], m_t[:, 1:2]))
                n = o.mark(V.tensor_copy(wa1[:, k, :], m_t[:, 0:1].to_broadcast([P, P])))
                dve.wait_ge(order, n)
            V.engine_nop().then_inc(S["weights_ready"], 1)
            for m in range(PAIRS):
                u = m % 2
                dve.wait_ge(xn_in[u], 16 * (m // 2 + 1))
                if m >= 2:
                    dve.wait_ge(S["hn_ready"], m - 1)
                dve.wait_ge(order, o.n)
                statistics(o, xn[u][:, 0, :], 0, u)
                statistics(o, xn[u][:, 1, :], 1, u, S["stats_ready"])
                if m >= 1:
                    normaliser(o, m - 1, 1 - u, slice(0, 2))
            normaliser(o, PAIRS - 1, 1, slice(0, 2))
            for a in range(2):
                first_words(o, a)
                first_nodes(o, a)
            chunk_max(o, 0, 0)
            chunk_max(o, 1, 0)
            end_order(o)

            def item_value(o, i, j, sweep):
                wait_apart(dve, "dve_passed", S["leaky_ready"], i)
                wait_apart(dve, "dve_passed", S["blocked_ready"], i + 1)
                dve.wait_ge(order, o.n)
                if sweep:
                    V.tensor_tensor(val[:, 0:HALF], nbt[:, HALF:N], s1_all[:, HALF:N], ALU.add
                                    ).then_inc(S["val_ready"], 1)
                    return
                n = o.mark(V.tensor_tensor_reduce(out=val[:, :], in0=nbt[:, :], in1=s1_all[:, :], scale=1.0,
                                                  scalar=-3e38, op0=ALU.add, op1=ALU.max, accum_out=m_t[:, 0:1]))
                dve.wait_ge(order, n)
                o.mark(V.tensor_scalar(m_t[:, 1:2], m_t[:, 0:1], SLOPE - 1, s2n[:, bass.ds(j, 1)], ALU.mult, ALU.add))
                n = o.mark(V.tensor_scalar(m_t[:, 2:3], m_t[:, 0:1], -SLOPE, None, ALU.mult))
                dve.wait_ge(order, n)
                V.scalar_tensor_tensor(out=nb[:, bass.ds(j, 1)], in0=m_t[:, 1:2], scalar=0.0, in1=m_t[:, 2:3],
                                       op0=ALU.min, op1=ALU.add).then_inc(S["val_ready"], 1)

            def item_leaky(o, i, w):
                dve.wait_ge(S["relu_ready"], i + 1)
                dve.wait_ge(order, o.n)
                V.scalar_tensor_tensor(out=lk[:, 0:w], in0=val[:, 0:w], scalar=SLOPE, in1=lk[:, 0:w],
                                       op0=ALU.mult, op1=ALU.add).then_inc(S["leaky_ready"], 1)

            def item_rows(o, i, j, jj, sweep):
                if sweep == 0:
                    dve.wait_ge(S["exp_ready"], i + 1)
                    dve.wait_ge(order, o.n)
                    n = o.mark(V.tensor_tensor(zs[:, :], za[jj][:, 0:1], za[jj][:, 1:2], ALU.add))
                    dve.wait_ge(order, n)
                    o.mark(V.reciprocal(rz[:, bass.ds(j, 1)], zs[:, :]))
                dve.wait_ge(S["av_done"], i)
                dve.wait_ge(order, o.n)
                V.tensor_scalar(hz[jj][:, :], h_all[:, bass.ds(j, 1), 0:C].rearrange("p a c -> p (a c)"),
                                rz[:, bass.ds(j, 1)], None, ALU.mult).then_inc(S["hz_ready"], 1)

            def flush(o, f):
                dve.wait_ge(S["gelu_done"], f + 1)
                dve.wait_ge(S["xo_in"], f * 16 + 16)
                dve.wait_ge(order, o.n)
                V.tensor_tensor(go[:, :, :], go[:, :, :], xo[:, :, :], ALU.add).then_inc(S["res_ready"], 1)

            def step(o, b, i, u, sweep, n, a, l, att, g):
                v = b * TILES + i * 2 + u
                it = (b - 1) * 32 + i * 4 + u * 2
                j = i * 4 + u * 2 - 16 * sweep
                w = N if sweep == 0 else HALF
                if l:
                    chunk_max(o, 2, v, u)
                if att:
                    item_value(o, it, j, sweep)
                if l:
                    dve.wait_ge(S["out0_done"], v + 1)
                    dve.wait_ge(l_in[u], (b * PAIRS + i) * 32 + 32)
                    dve.wait_ge(x1_stored[u], (b * PAIRS + i) * 16)
                    dve.wait_ge(order, o.n)
                    x1_made = o.mark(V.scalar_tensor_tensor(out=x1[u][:, :], in0=ps_l[:, 0:C], scalar=0.0,
                                                            in1=xl[u][:, :], op0=ALU.max, op1=ALU.add))
                    if n:
                        m = (b + 1) * PAIRS + i * 2 + u
                        dve.wait_ge(xn_in[u], (b + 1) * 64 + i * 16 + 16)
                        dve.wait_ge(S["hn_ready"], m - 1)
                        dve.wait_ge(order, o.n)
                        statistics(o, xn[u][:, 0, :], 0, u)
                        statistics(o, xn[u][:, 1, :], 1, u)
                    dve.wait_ge(order, o.n)
                    statistics(o, x1[u][:, :], 2, u, S["stats_ready"])
                if att:
                    item_leaky(o, it, w)
                    item_value(o, it + 1, j + 1, sweep)
                if g:
                    chunk_max(o, 0, v + 1)
                if l:
                    normaliser(o, PAIRS + v, u, slice(0 if n else 2, 3))
                    dve.wait_ge(S["norm_ready"], PAIRS + v + 1)
                    dve.wait_ge(order, o.n)
                    V.tensor_scalar(y1[:, :], x1[u][:, :], rs[u][:, 2:3], nmr[u][:, 2:3], ALU.mult, ALU.add
                                    ).then_inc(S["y1_ready"], 1)
                if a:
                    first_words(o, v + 2)
                if att:
                    item_rows(o, it, j, 0, sweep)
                    item_leaky(o, it + 1, w)
                if a:
                    first_nodes(o, u)
                if g:
                    chunk_max(o, 1, v + 1)
                if att:
                    item_rows(o, it + 1, j + 1, 1, sweep)

            def hand_over(o, b):
                dve.wait_ge(S["h_saved"], b * TILES)
                dve.wait_ge(order, o.n)
                o.mark(V.tensor_scalar(s2p[:, :], h_acc[:, :, C], 1 - SLOPE, None, ALU.mult))
                o.mark(V.tensor_scalar(s2n[:, :], h_acc[:, :, C], SLOPE - 1, None, ALU.mult))
                V.tensor_copy(s1_all[:, :], s1_acc[:, :]).then_inc(S["s1_copied"], 1)
                wait_apart(dve, "dve_passed", S["s1_copied"], b)
                wait_apart(dve, "dve_passed", S["h_copied"], b)

            def round_(b, first=False, last=False, drain=False):
                if not first:
                    o = Order(order)
                    hand_over(o, b)
                    end_order(o)
                for sweep in range(2):
                    def pair(i, a=True, g=(True, True)):
                        o = Order(order)
                        for u in range(2):
                            step(o, b, i, u, sweep, n=sweep == 0 and not last and not drain, a=a and not drain,
                                 l=not drain, att=not first, g=g[u] and not drain)
                        end_order(o)
                    i0 = sweep * 4
                    pair(i0)
                    if not first and not (type(b) is int and b == 1 and sweep == 0):
                        o = Order(order)
                        flush(o, b * 2 - 3 + sweep)
                    with dve.Fori(i0 + 1, i0 + 4 - sweep) as i:
                        pair(i)
                    if sweep:
                        pair(i0 + 3, a=not last, g=(True, not last))

            round_(0, first=True)
            round_(1)
            with dve.Fori(2, NB - 1) as b:
                round_(b)
            round_(NB - 1, last=True)
            round_(NB, drain=True)
            flush(Order(order), 2 * NB - 1)

        @block.tensor
        def _(pe):
            T = nc.tensor

            def transpose_signs(a):
                pe.wait_ge(S["signed"], a + 1)
                pe.wait_ge(S["edges_ready"], a)
                pe.wait_ge(S["words_read"], a)
                for m in range(TILES):
                    ins = T.transpose(sgt[:, m * P:(m + 1) * P], sg[:, m * P:(m + 1) * P], identb)
                ins.then_inc(S["signs_transposed"], 1)

            def make_words(a):
                pe.wait_ge(S["bits_ready"], a + 1)
                pe.wait_ge(S["edges_ready"], a + 1)
                for m in range(TILES):
                    ins = T.matmul(words[:, m * 16:(m + 1) * 16], bits[:, m, :], pack, start=True, stop=True)
                ins.then_inc(S["words_done"], 1)

            def av(i, jj):
                pe.wait_ge(S["exp_ready"], i + 1)
                pe.wait_ge(S["hz_ready"], i + 1)
                for k in range(8):
                    ins = T.matmul(ps_av[:, k * C:(k + 1) * C], ex[jj][:, k * P:(k + 1) * P], hz[jj][:, :],
                                   start=False, stop=False)
                ins.then_inc(S["av_done"], 1)

            def open_sweep(f):
                if not (type(f) is int and f == 0):
                    pe.wait_ge(S["gelu_done"], f)
                for k in range(4):
                    T.matmul(ps_av[:, k * 512:(k + 1) * 512], zeros[0:1, 0:P], zeros[0:1, :], start=True, stop=False)

            def close_sweep():
                for k in range(4):
                    ins = T.matmul(ps_av[:, k * 512:(k + 1) * 512], zeros[0:1, 0:P], zeros[0:1, :], start=False, stop=True)
                ins.then_inc(S["sweep_done"], 1)

            def step(b, i, u, a, l, att, fo=None):
                v = b * TILES + i * 2 + u
                it = (b - 1) * 32 + i * 4 + u * 2
                if l:
                    pe.wait_ge(l_in[u], (b * PAIRS + i) * 32 + 32)
                    pe.wait_ge(maxed[2], v + 2)
                    for k in range(4):
                        ins = T.transpose(ps_t[:, k * P:(k + 1) * P], hl[u][:, k // 2, k % 2 * P:(k % 2 + 1) * P], ident)
                    ins.then_inc(S["cat_transposed"], 1)
                if a:
                    transpose_signs(v + 2)
                if l:
                    pe.wait_ge(S["cat_ready"], v + 1)
                    pe.wait_ge(S["h_saved"], v)
                    for k in range(4):
                        T.matmul(ps_l[:, 0:C], hcat[:, k, :], w0[:, k, :], start=k == 0, stop=False)
                    T.matmul(ps_l[:, 0:C], ones[:, :], bias0[:, :], start=False, stop=True).then_inc(S["out0_done"], 1)
                if a:
                    make_words(v + 2)
                if fo is not None:
                    open_sweep(fo)
                if att:
                    av(it, 0)
                if l:
                    pe.wait_ge(S["y1_ready"], v + 1)
                    for k in range(2):
                        ins = T.transpose(ps_t[:, k * P:(k + 1) * P], y1[:, k * P:(k + 1) * P], ident)
                    ins.then_inc(S["y1_transposed"], 1)
                    pe.wait_ge(S["h1t_ready"], v + 1)
                    for k in range(2):
                        T.matmul(ps_l[:, 0:C + 1], h1t[:, k, :], w1[:, k, :], start=k == 0, stop=k == 1)
                    for k in range(2):
                        ins = T.matmul(ps_l[:, 384:384 + P], wa1[:, k, :], h1t[:, k, :], start=k == 0, stop=k == 1)
                    ins.then_inc(S["h_done"], 1)
                if att:
                    av(it + 1, 1)

            pe.sem_inc(S["av_done"], 1)
            pe.wait_ge(S["consts_in"], 16 * 6)
            pe.wait_ge(S["ones_ready"], 3)
            pe.wait_ge(S["weights_ready"], 1)
            for a in range(2):
                transpose_signs(a)
                make_words(a)

            def round_(b, first=False, last=False, drain=False):
                for sweep in range(2):
                    def pair(i, a=True, fo=None):
                        for u in range(2):
                            step(b, i, u, a=a and not drain, l=not drain, att=not first, fo=fo if u == 0 else None)
                    i0 = sweep * 4
                    end = i0 + 4 - (last and sweep)
                    pair(i0, fo=None if first else b * 2 - 2 + sweep)
                    with pe.Fori(i0 + 1, end) as i:
                        pair(i)
                    if last and sweep:
                        pair(i0 + 3, a=False)
                    if not first:
                        close_sweep()

            round_(0, first=True)
            round_(1)
            with pe.Fori(2, NB - 1) as b:
                round_(b)
            round_(NB - 1, last=True)
            round_(NB, drain=True)


def constants():
    import numpy as np
    f = np.zeros((P, C_COLS), np.float32)
    f[:, C_ID:C_ID + P] = np.eye(P)
    f[:, C_KEY:C_KEY + WORDS] = (WORDS - np.arange(WORDS)) * (1 << WORD)
    f[:, C_IOTA:C_IOTA + WORD] = np.arange(WORD)
    for m in range(P):
        f[m, C_PACK + m // WORD] = 2.0 ** (WORD - 1 - m % WORD)
    i = np.zeros((P, WORD), np.int32)
    i[:, :] = 1 << (WORD - 1 - np.arange(WORD))
    return {"const_f": f, "const_i": i}


def kernel(x, adj, L0_gnn_W, L0_gnn_b, L1_gnn_W, L1_gnn_a):
    import numpy as np
    import concourse.bacc as bacc
    from concourse.bass_utils import run_bass_kernel_spmd

    nc = bacc.Bacc("TRN2", target_bir_lowering=False, num_devices=1)
    given = {"x": x, "adj": adj, "L0_gnn_W": L0_gnn_W, "L0_gnn_b": L0_gnn_b, "L1_gnn_W": L1_gnn_W,
             "L1_gnn_a": L1_gnn_a, **constants()}
    arrays = {f"in_{k}": np.ascontiguousarray(v) for k, v in given.items()}
    args = [nc.dram_tensor(k, a.shape, mybir.dt.from_np(a.dtype), kind="ExternalInput").ap() for k, a in arrays.items()]
    out = nc.dram_tensor("out_0", (NB, N, C), fp32, kind="ExternalOutput").ap()
    graph_layers(nc, *args, out)
    return run_bass_kernel_spmd(nc, [arrays], core_ids=[0]).results[0]["out_0"]
```

```python
from contextlib import ExitStack

import concourse.bass as bass
from concourse import mybir

fp32 = mybir.dt.float32
bf16 = mybir.dt.bfloat16
i32 = mybir.dt.int32
u8 = mybir.dt.uint8
ALU = mybir.AluOpType
ACT = mybir.ActivationFunctionType
AX = mybir.AxisListType

P = 128
NB, N, C = 8, 2048, 256
TILES = N // P
HALF = N // 2
KEEP = 25
ROWS = N + 1
WORD = 8
WORDS = N // WORD
CHUNKS = (9, 8, 8)
PAIRS = TILES // 2
EPS = 1e-5
SLOPE = 0.4
BLOCKED = 1e30

C_ID, C_PACK, C_KEY, C_IOTA = 0, P, P + 16, P + 16 + WORDS
C_COLS = C_IOTA + WORD


class Order:

    def __init__(self, sem):
        self.sem, self.n = sem, 0

    def mark(self, instruction):
        instruction.then_inc(self.sem, 1)
        self.n += 1
        return self.n


def graph_layers(nc, x, adj, W0, b0, W1, a1, const_f, const_i, out):
    ctx = ExitStack()
    with ctx:
        def sb(name, shape, dt):
            return ctx.enter_context(nc.sbuf_tensor(name, shape, dt))

        def ps(name, shape, dt):
            return ctx.enter_context(nc.psum_tensor(name, shape, dt))

        def sem(name):
            return ctx.enter_context(nc.semaphore(name))

        table = [nc.dram_tensor(f"h_table{u}", (ROWS, C), fp32).ap() for u in range(2)]
        edges_t = nc.dram_tensor("edges_t", (NB * N, N), u8).ap()
        x1_dram = nc.dram_tensor("x1_rows", (NB * N, C), fp32).ap()
        x_rows = x.rearrange("b n c -> (b n) c")
        adj_rows = adj.rearrange("b n m -> (b n) m")
        out_rows = out.rearrange("b n c -> (b n) c")

        cf = sb("cf", [P, C_COLS], fp32)
        cb = sb("cb", [P, P + 16], bf16)
        ci = sb("ci", [P, WORD], i32)
        ident, identb, pack = cf[:, C_ID:C_ID + P], cb[:, 0:P], cb[:, P:P + 16]
        w0 = sb("w0", [P, 4, C], fp32)
        w1 = sb("w1", [P, 2, C + 1], fp32)
        wa1 = sb("wa1", [P, 2, P], fp32)
        bias0 = sb("bias0", [1, C], fp32)
        ones = sb("ones", [1, P], fp32)
        zeros = sb("zeros", [1, 512], bf16)
        zrow = sb("zrow", [1, C], fp32)

        xn = [sb(f"xn{u}", [P, 2, C], fp32) for u in range(2)]
        bn6 = sb("bn6", [P, 3, 6], fp32)
        mv = [sb(f"mv{u}", [P, 3, 2], fp32) for u in range(2)]
        std = [sb(f"std{u}", [P, 3], fp32) for u in range(2)]
        rs = [sb(f"rs{u}", [P, 3], fp32) for u in range(2)]
        nmr = [sb(f"nmr{u}", [P, 3], fp32) for u in range(2)]
        lt = sb("lt", [P, 2, 3], fp32)
        ad = [sb(f"ad{u}", [P, N], i32) for u in range(2)]
        sg = sb("sg", [P, N], bf16)
        bits = sg[:, :].rearrange("p (m n) -> p m n", n=P)
        stage = sb("stage", [P, TILES, 8 * P], u8)
        wv = sb("wv", [P, WORDS], fp32)
        wt = sb("wt", [P, WORDS], fp32)
        top = sb("top", [P, 32], fp32)
        topi = sb("topi", [P, KEEP], i32)
        hi = sb("hi", [P, KEEP], i32)
        bt = sb("bt", [P, KEEP, WORD], i32)
        cand = sb("cand", [P, KEEP, WORD], fp32)
        cand2 = sb("cand2", [P, KEEP, WORD], fp32)
        top2 = sb("top2", [P, 32], fp32)
        idx = [sb(f"idx{u}", [P, KEEP], i32) for u in range(2)]
        gb = [sb(f"gb{c}", [P, n + (c > 0), C], fp32) for c, n in enumerate(CHUNKS)]
        xl = [sb(f"xl{u}", [P, C], fp32) for u in range(2)]
        hl = [sb(f"hl{u}", [P, 2, C], fp32) for u in range(2)]
        hcat = sb("hcat", [P, 4, P], fp32)
        x1 = [sb(f"x1_{u}", [P, C], fp32) for u in range(2)]
        y1 = sb("y1", [P, C], fp32)
        h1t = sb("h1t", [P, 2, P], fp32)
        h_acc = sb("h_acc", [P, TILES, C + 1], fp32)
        s1_acc = sb("s1_acc", [P, N], fp32)
        h_all = sb("h_all", [P, TILES, C + 1], fp32)
        s1_all = sb("s1_all", [P, N], fp32)
        s2p = sb("s2p", [P, TILES], fp32)
        s2n = sb("s2n", [P, TILES], fp32)
        edge = [sb(f"edge{u}", [P, 2, N], u8) for u in range(2)]
        nbt = sb("nbt", [P, N], bf16)
        val = [sb(f"val{u}", [P, N], fp32) for u in range(2)]
        lk = sb("lk", [P, N], fp32)
        ex = [sb(f"ex{u}", [P, HALF], fp32) for u in range(2)]
        hz = [sb(f"hz{u}", [P, C], fp32) for u in range(2)]
        m_t = sb("m_t", [P, 3], fp32)
        nb = sb("nb", [P, TILES], fp32)
        za = [sb(f"za{u}", [P, 2], fp32) for u in range(2)]
        zs = sb("zs", [P, 1], fp32)
        rz = sb("rz", [P, TILES], fp32)
        xo = sb("xo", [P, 8, C], fp32)
        go = sb("go", [P, 8, C], fp32)

        ps_av = ps("ps_av", [P, 8 * C], fp32)
        ps_c = ps("ps_c", [P, 1024], fp32)
        ps_t = ps("ps_t", [P, 512], fp32)
        ps_l = ps("ps_l", [P, 512], fp32)
        sgt = ps_c[:, :].bitcast(bf16)
        words = ps_c[:, 0:WORDS]

        S = {n: sem(n) for n in (
            "consts_in", "weights_ready", "ones_ready", "zrow_stored",
            "signed", "signs_transposed", "bits_ready", "edges_ready", "edges_stored", "words_done", "words_read",
            "idx_ready", "stats_ready", "std_ready", "norm_ready", "hn_ready",
            "agg_ready", "cat_transposed", "cat_ready", "out0_done", "y1_ready", "y1_transposed", "h1t_ready",
            "h_done", "h_saved", "h_copied", "s1_copied",
            "blocked_ready", "val_ready", "relu_ready", "leaky_ready", "exp_ready", "hz_ready", "av_done",
            "sweep_done", "gelu_done", "xo_in", "res_ready", "out_stored", "order",
            "sp_passed", "pool_passed", "dve_passed")}
        adj_in = [sem(f"adj_in{u}") for u in range(2)]
        xn_in = [sem(f"xn_in{u}") for u in range(2)]
        hn_stored = [sem(f"hn_stored{u}") for u in range(2)]
        l_in = [sem(f"l_in{u}") for u in range(2)]
        x1_stored = [sem(f"x1_stored{u}") for u in range(2)]
        edge_in = [sem(f"edge_in{u}") for u in range(2)]
        gathered = [sem(f"gathered{c}") for c in range(3)]
        maxed = [sem(f"maxed{c}") for c in range(3)]

        def lk_of(jj, drain):
            return gb[0][:, 0:8, :].rearrange("p k c -> p (k c)") if drain and jj else lk

        SECTIONS = {False: [(0, 0, 1), (2, 1, 4), (8, 4, 5), (10, 5, 7), (14, 7, 8)],
                    True: [(0, 0, 1), (2, 1, 4), (8, 4, 5), (10, 5, 6), (12, 6, 7), (14, 7, 8)]}

        def wait_apart(engine, name, semaphore, value):
            engine.wait_ge(semaphore, value)
            engine.sem_inc(S[name], 1)

        block = ctx.enter_context(nc.Block())

        @block.sync
        def _(sp):
            def load_adj(a, u):
                sp.dma_start(ad[u][:, :], adj_rows[bass.ds(a * P, P), :]).then_inc(adj_in[u], 16)

            def load_xn(m, u):
                sp.dma_start(xn[u][:, :, :], x_rows[bass.ds(m * 2 * P, 2 * P), :].rearrange("(k p) c -> p k c", p=P)
                             ).then_inc(xn_in[u], 16)

            def store_hn(tb, k, m, u):
                wait_apart(sp, "sp_passed", S["hn_ready"], m + 1)
                sp.dma_start(table[tb][k * 2 * P:(k + 1) * 2 * P, :].rearrange("(k p) c -> p k c", p=P),
                             xn[u][:, :, :]).then_inc(hn_stored[u], 16)

            def load_l(tb, b, t, u):
                sp.dma_start(xl[u][:, :], x_rows[bass.ds(b * N + t * P, P), :]).then_inc(l_in[u], 16)
                sp.dma_start(hl[u][:, 0, :], table[tb][t * P:(t + 1) * P, :]).then_inc(l_in[u], 16)

            def load_edge(bt_, t, u):
                sp.dma_start(edge[u][:, :, :], edges_t[bass.ds(bt_ * N + (t % 8) * 2 * P, 2 * P), :]
                             .rearrange("(k p) n -> p k n", p=P)).then_inc(edge_in[u], 16)

            sp.dma_start(cf[:, :], const_f).then_inc(S["consts_in"], 16)
            load_xn(0, 0)
            load_xn(1, 1)
            load_adj(0, 0)
            load_adj(1, 1)
            sp.dma_start(ci[:, :], const_i).then_inc(S["consts_in"], 16)
            sp.dma_start(w0[:, :, :], W0.rearrange("(k p) o -> p k o", p=P)).then_inc(S["consts_in"], 16)
            sp.dma_start(w1[:, :, 0:C], W1.rearrange("(k p) o -> p k o", p=P)).then_inc(S["consts_in"], 16)
            sp.dma_start(bias0[:, :], b0.rearrange("(a o) -> a o", a=1)).then_inc(S["consts_in"], 16)
            sp.dma_start(val[0][:, 0:2 * C], a1.rearrange("f a -> a f").partition_broadcast(P)
                         if False else a1.rearrange("f a -> a f").to_broadcast([P, 2 * C])).then_inc(S["consts_in"], 16)
            sp.sem_inc(S["edges_stored"], 16)
            for m in range(PAIRS):
                store_hn(0, m, m, m % 2)
                if m + 2 < PAIRS:
                    wait_apart(sp, "sp_passed", hn_stored[m % 2], 16 * (m // 2 + 1))
                    load_xn(m + 2, m % 2)
                if m % 2:
                    a = m // 2
                    wait_apart(sp, "sp_passed", S["signed"], a + 1)
                    load_adj(2 + a, a % 2)
            wait_apart(sp, "sp_passed", S["ones_ready"], 1)
            for tb in range(2):
                sp.dma_start(table[tb][N:ROWS, :], zrow[:, :]).then_inc(S["zrow_stored"], 16)
            for u in range(2):
                wait_apart(sp, "sp_passed", hn_stored[u], 16 * PAIRS // 2)
            load_l(0, 0, 0, 0)

            def store_edges(b, q):
                g4 = b * 4 + q
                wait_apart(sp, "sp_passed", S["edges_ready"], g4 * 4 + 4)
                wait_apart(sp, "sp_passed", S["edges_stored"], g4 * 16 + 16)
                at = 4 * P * (q % 2)
                sp.dma_start(edges_t.rearrange("(b m p) n -> b p m n", p=P, m=TILES)[bass.ds(b, 1)]
                             .rearrange("b p m n -> p (b m) n")[:, :, q * 4 * P:(q + 1) * 4 * P],
                             stage[:, :, at:at + 4 * P]).then_inc(S["edges_stored"], 16)

            store_edges(0, 0)

            def step(b, tb, t, n, a, l, e, w, last):
                v = b * TILES + t
                u = t % 2
                if n:
                    m = (b + 1) * PAIRS + t
                    wait_apart(sp, "sp_passed", hn_stored[u], (b + 1) * 64 + t // 2 * 16)
                    load_xn(m, u)
                if e:
                    nt = (t + 1) % 16
                    eb = b - 1 + (t + 1) // 16
                    if t == 15:
                        wait_apart(sp, "sp_passed", S["edges_stored"], 16 * 4 * eb + 16 * 5)
                    if w:
                        wait_apart(sp, "sp_passed", S["blocked_ready"], (b - 1) * 32 + 2 * t)
                    load_edge(eb, nt, nt % 2)
                if l and not (type(b) is int and b == NB - 1 and t == 15):
                    wait_apart(sp, "sp_passed", S["cat_transposed"], v)
                    wait_apart(sp, "sp_passed", S["stats_ready"], PAIRS + v)
                    if t == 15:
                        for k in range(2):
                            wait_apart(sp, "sp_passed", hn_stored[k], b * 64 + 128)
                        load_l(1 - tb, b + 1, 0, 0)
                    else:
                        load_l(tb, b, t + 1, (t + 1) % 2)
                if a:
                    wait_apart(sp, "sp_passed", S["signed"], v + 5)
                    load_adj(v + 6, u)
                if l:
                    wait_apart(sp, "sp_passed", S["stats_ready"], PAIRS + v + 1)
                    sp.dma_start(x1_dram[bass.ds(v * P, P), :], x1[u][:, :]).then_inc(x1_stored[u], 16)
                if n:
                    if t == 0:
                        wait_apart(sp, "sp_passed", maxed[2], b * TILES + 1)
                        wait_apart(sp, "sp_passed", S["cat_transposed"], b * TILES)
                    store_hn(1 - tb, t, m, u)
                if t % 4 == 3 and l and not (last and t == 15):
                    store_edges(b + (t + 1) // 16, (t + 1) // 4 % 4)

            def load_xo(bt_, h, f):
                wait_apart(sp, "sp_passed", S["res_ready"], f)
                for u in range(2):
                    wait_apart(sp, "sp_passed", x1_stored[u], bt_ * 128 + 128)
                sp.dma_start(xo[:, :, :], x1_dram[bass.ds(bt_ * N + h * HALF, HALF), :]
                             .rearrange("(k p) c -> p k c", p=P)).then_inc(S["xo_in"], 16)

            def store_out(bt_, h, f):
                wait_apart(sp, "sp_passed", S["res_ready"], f + 1)
                sp.dma_start(out_rows[bass.ds(bt_ * N + h * HALF, HALF), :].rearrange("(k p) c -> p k c", p=P),
                             go[:, :, :]).then_inc(S["out_stored"], 16)

            def round_(b, tb, first=False, last=False, drain=False):
                for t in range(TILES):
                    step(b, tb, t, n=t < 8 and not last and not drain, a=not drain and not (last and t >= 10),
                         l=not drain, e=(not first or t == 15) and not (drain and t == 15), w=not first and not (type(b) is int and b == 1 and t == 0), last=last)
                    if not first:
                        if t == 3:
                            if not (type(b) is int and b == 1):
                                store_out(b - 2, 1, b * 2 - 3)
                            load_xo(b - 1, 0, b * 2 - 2)
                        if t == 11:
                            store_out(b - 1, 0, b * 2 - 2)
                            load_xo(b - 1, 1, b * 2 - 1)

            round_(0, 0, first=True)
            round_(1, 1)
            with sp.Fori(2, NB - 2, 2) as b:
                round_(b, 0)
                round_(b + 1, 1)
            round_(NB - 2, 0)
            round_(NB - 1, 1, last=True)
            round_(NB, 0, drain=True)
            store_out(NB - 1, 1, 2 * NB - 1)
            wait_apart(sp, "sp_passed", S["out_stored"], 16 * 2 * NB)

        @block.gpsimd
        def _(pool):
            nc.gpsimd.memset(zeros[:, :], 0.0).then_inc(S["ones_ready"], 2)
            pool.wait_ge(S["zrow_stored"], 32)
            with pool.Fori(0, NB, 2) as b2:
                for tb in range(2):
                    b = b2 + tb
                    for u in range(2):
                        wait_apart(pool, "pool_passed", hn_stored[u], b * 64 + 64)
                    with pool.Fori(0, PAIRS) as i:
                        for u in range(2):
                            g = b * TILES + i * 2 + u
                            wait_apart(pool, "pool_passed", S["idx_ready"], g + 1)
                            k = 0
                            for c, n in enumerate(CHUNKS):
                                wait_apart(pool, "pool_passed", maxed[c], g + 1)
                                for s in range(n):
                                    pool.indirect_dma_start(gb[c][:, s + (c > 0), :], None, table[tb],
                                                            bass.IndirectOffsetOnAxis(idx[u][:, k:k + 1], 0)
                                                            ).then_inc(gathered[c], 16)
                                    k += 1

        @block.scalar
        def _(act):

            def sign(k, a, u):
                act.wait_ge(adj_in[u], k * 16 + 16)
                act.wait_ge(S["words_done"], a)
                nc.scalar.activation(sg[:, :], ad[u][:, :], ACT.Sign).then_inc(S["signed"], 1)

            def evacuate_signs(a, col):
                act.wait_ge(S["signs_transposed"], a + 1)
                nc.scalar.activation(bits, sgt.rearrange("p (m n) -> p m n", n=P), ACT.Square).then_inc(S["bits_ready"], 1)
                act.wait_ge(S["edges_stored"], a // 4 * 16)
                nc.scalar.activation(stage[:, :, bass.ds(col, P)], sgt.rearrange("p (m n) -> p m n", n=P), ACT.Relu
                                     ).then_inc(S["edges_ready"], 1)

            def root(q, u, cols):
                act.wait_ge(S["stats_ready"], q + 1)
                nc.scalar.activation(std[u][:, cols], mv[u][:, cols, 1], ACT.Sqrt, bias=EPS).then_inc(S["std_ready"], 1)

            def norm_pair(q, m, u):
                act.wait_ge(S["norm_ready"], q + 1)
                for k in range(2):
                    ins = nc.scalar.activation(xn[u][:, k, :], xn[u][:, k, :], ACT.Relu,
                                               bias=nmr[u][:, k:k + 1], scale=rs[u][:, k:k + 1])
                ins.then_inc(S["hn_ready"], 1)

            act.wait_ge(S["consts_in"], 16 * 6)
            for m in range(PAIRS):
                u = m % 2
                act.wait_ge(xn_in[u], 16 * (m // 2 + 1))
                root(m, u, slice(0, 2))
                norm_pair(m, m, u)
                if m % 2:
                    sign(m // 4, m // 2, m // 2 % 2)
                    evacuate_signs(m // 2, m // 2 * P)

            def blocked(i, k, jj, u, cols):
                act.wait_ge(edge_in[u], k * 16 + 16)
                act.wait_ge(S["val_ready"], i)
                nc.scalar.activation(nbt[:, cols], edge[u][:, jj, cols], ACT.Identity, scale=BLOCKED, bias=-BLOCKED
                                     ).then_inc(S["blocked_ready"], 1)

            def relu_part(i, j, jj, sweep, drain):
                w = HALF if sweep else N
                act.wait_ge(S["val_ready"], i + 1)
                act.wait_ge(S["exp_ready"], i - drain)
                nc.scalar.activation(lk_of(jj, drain)[:, 0:w], val[jj][:, 0:w], ACT.Relu, scale=1 - SLOPE,
                                     bias=s2p[:, bass.ds(j, 1)]).then_inc(S["relu_ready"], 1)

            def exp_part(i, j, jj, sweep, drain):
                act.wait_ge(S["leaky_ready"], i + 1)
                act.wait_ge(S["av_done"], i)
                bias, q = nb[:, bass.ds(j, 1)], lk_of(jj, drain)
                if sweep == 0:
                    nc.scalar.activation(ex[jj][:, :], q[:, 0:HALF], ACT.Exp, bias=bias, accum_out=za[jj][:, 0:1])
                    nc.scalar.activation(q[:, HALF:N], q[:, HALF:N], ACT.Exp, bias=bias, accum_out=za[jj][:, 1:2]
                                         ).then_inc(S["exp_ready"], 1)
                else:
                    nc.scalar.activation(ex[jj][:, :], q[:, 0:HALF], ACT.Exp, bias=bias).then_inc(S["exp_ready"], 1)

            def flush(f):
                act.wait_ge(S["sweep_done"], f + 1)
                act.wait_ge(S["out_stored"], f * 16)
                nc.scalar.activation(go[:, :, :], ps_av[:, :].rearrange("p (k c) -> p k c", c=C), ACT.Gelu
                                     ).then_inc(S["gelu_done"], 1)

            def step(b, i, u, t, n, a, l, new, old, fl, drain):
                v = b * TILES + i * 2 + u
                k = b * PAIRS + i
                it = (b - 1) * 32 + i * 4 + u * 2
                sweep, before = t // 8 % 2, (t - 1) // 8 % 2
                j = i * 4 + u * 2 - 16 * sweep
                j1 = j - 1 if t % 8 else 15
                j2 = j - 2 if t % 8 else 14
                cols = slice(HALF, N) if sweep else slice(0, N)
                if new:
                    blocked(it, k - PAIRS, 0, u, cols)
                if fl is not None:
                    flush(fl)
                if old:
                    exp_part(it - 2, j2, 0, before, drain)
                if l:
                    act.wait_ge(S["cat_transposed"], v + 1)
                    nc.scalar.copy(hcat[:, :, :], ps_t[:, :].rearrange("p (k n) -> p k n", n=P)).then_inc(S["cat_ready"], 1)
                if old:
                    relu_part(it - 1, j1, 1, before, drain)
                if a:
                    sign(k + 2, v + 4, u)
                if new:
                    blocked(it + 1, k - PAIRS, 1, u, cols)
                if l:
                    root(PAIRS + v, u, slice(0 if n else 2, 3))
                if a:
                    evacuate_signs(v + 4, (v + 4) % 8 * P)
                if l:
                    act.wait_ge(S["y1_transposed"], v + 1)
                    nc.scalar.activation(h1t[:, :, :], ps_t[:, 0:C].rearrange("p (k n) -> p k n", n=P), ACT.Relu
                                         ).then_inc(S["h1t_ready"], 1)
                if old:
                    exp_part(it - 1, j1, 1, before, drain)
                if t == 0 and new:
                    act.wait_ge(S["h_saved"], b * TILES)
                    act.wait_ge(S["hz_ready"], (b - 1) * 32)
                    nc.scalar.copy(h_all[:, :, :], h_acc[:, :, :]).then_inc(S["h_copied"], 1)
                if l:
                    act.wait_ge(S["h_done"], v + 1)
                    if not (type(b) is int and b == 0):
                        act.wait_ge(S["s1_copied"], b)
                        act.wait_ge(S["h_copied"], b)
                    nc.scalar.copy(h_acc[:, bass.ds(i * 2 + u, 1), :].rearrange("p a c -> p (a c)"), ps_l[:, 0:C + 1])
                    nc.scalar.copy(s1_acc[:, bass.ds((i * 2 + u) * P, P)], ps_l[:, 384:384 + P]).then_inc(S["h_saved"], 1)
                if new:
                    relu_part(it, j, 0, sweep, drain)
                if n:
                    norm_pair(PAIRS + v, (b + 1) * PAIRS + i * 2 + u, u)

            def round_(b, first=False, last=False, drain=False):
                def pair(i, t0):
                    for u in range(2):
                        t = t0 + u
                        one = type(b) is int and b == 1
                        fl = {1: b * 2 - 3, 9: b * 2 - 2}.get(t) if not first and not (one and t == 1) else None
                        step(b, i, u, t, n=t < 8 and not last and not drain, a=not drain and not (last and t >= 12),
                             l=not drain, new=not first, old=not first and not (one and t == 0), fl=fl, drain=drain)
                for t0, i0, end in SECTIONS[last]:
                    if end == i0 + 1:
                        pair(i0, t0)
                    else:
                        with act.Fori(i0, end) as i:
                            pair(i, t0)

            round_(0, first=True)
            round_(1)
            with act.Fori(2, NB - 1) as b:
                round_(b)
            round_(NB - 1, last=True)
            round_(NB, drain=True)
            step(NB + 1, 0, 0, 0, n=False, a=False, l=False, new=False, old=True, fl=None, drain=True)
            flush(2 * NB - 1)

        @block.vector
        def _(dve):
            order = S["order"]
            V = nc.vector

            def end_order(o):
                dve.wait_ge(order, o.n)
                dve.sem_clear(order)

            def statistics(o, src, slot, u, ready=None):
                n = o.mark(V.bn_stats(bn6[:, slot, :], src))
                dve.wait_ge(order, n)
                ins = V.bn_aggr(mv[u][:, slot, :], bn6[:, slot, :])
                if ready is not None:
                    ins.then_inc(ready, 1)
                else:
                    o.mark(ins)

            def normaliser(o, q, u, cols):
                mean, var = mv[u][:, cols, 0], mv[u][:, cols, 1]
                dve.wait_ge(S["std_ready"], q + 1)
                dve.wait_ge(order, o.n)
                n = o.mark(V.reciprocal(rs[u][:, cols], std[u][:, cols]))
                dve.wait_ge(order, n)
                n = o.mark(V.tensor_tensor(lt[:, 0, cols], rs[u][:, cols], rs[u][:, cols], ALU.mult))
                dve.wait_ge(order, n)
                n = o.mark(V.scalar_tensor_tensor(out=lt[:, 1, cols], in0=var, scalar=EPS, in1=lt[:, 0, cols],
                                                  op0=ALU.add, op1=ALU.mult))
                dve.wait_ge(order, n)
                n = o.mark(V.tensor_scalar(lt[:, 0, cols], lt[:, 1, cols], -0.5, 1.5, ALU.mult, ALU.add))
                dve.wait_ge(order, n)
                n = o.mark(V.tensor_tensor(rs[u][:, cols], rs[u][:, cols], lt[:, 0, cols], ALU.mult))
                dve.wait_ge(order, n)
                V.scalar_tensor_tensor(out=nmr[u][:, cols], in0=mean, scalar=-1.0, in1=rs[u][:, cols],
                                       op0=ALU.mult, op1=ALU.mult).then_inc(S["norm_ready"], 1)

            def read_words(o, a):
                dve.wait_ge(S["words_done"], a + 1)
                n = o.mark(V.scalar_tensor_tensor(out=wt[:, :], in0=words, scalar=0.0, in1=cf[:, C_KEY:C_KEY + WORDS],
                                                  op0=ALU.is_gt, op1=ALU.mult))
                dve.wait_ge(order, n)
                V.tensor_tensor(wv[:, :], wt[:, :], words, ALU.add).then_inc(S["words_read"], 1)

            def search(o, a, u, find_words, find_nodes):
                nodes = cand[:, :, :].rearrange("p k w -> p (k w)")
                work = cand2[:, :, :].rearrange("p k w -> p (k w)")
                nw = nn = o.n
                if find_words:
                    wait_apart(dve, "dve_passed", S["words_read"], a + 1)
                if find_nodes:
                    dve.wait_ge(order, nn)
                    nn = o.mark(V.tensor_tensor(cand2[:, :, :], hi[:, :].unsqueeze(2).to_broadcast([P, KEEP, WORD]),
                                                cf[:, C_IOTA:C_IOTA + WORD].unsqueeze(1).to_broadcast([P, KEEP, WORD]),
                                                ALU.subtract))
                if find_words:
                    dve.wait_ge(order, nw)
                    nw = o.mark(V.max(top[:, 0:8], wv[:, :]))
                if find_nodes:
                    dve.wait_ge(order, nn)
                    nn = o.mark(V.scalar_tensor_tensor(out=cand[:, :, :], in0=bt[:, :, :], scalar=0.0,
                                                       in1=cand2[:, :, :], op0=ALU.is_gt, op1=ALU.mult))
                if find_words:
                    dve.wait_ge(order, nw)
                    nw = o.mark(V.match_replace(wt[:, :], top[:, 0:8], wv[:, :], 0.0))
                if find_nodes:
                    dve.wait_ge(order, nn)
                    nn = o.mark(V.max(top2[:, 0:8], nodes))
                for r in range(1, 4):
                    if find_words:
                        dve.wait_ge(order, nw)
                        nw = o.mark(V.max(top[:, 8 * r:8 * r + 8], wt[:, :]))
                    if find_nodes:
                        dve.wait_ge(order, nn)
                        nn = o.mark(V.match_replace(work, top2[:, 8 * r - 8:8 * r], nodes if r == 1 else work, 0.0))
                    if find_words and r < 3:
                        dve.wait_ge(order, nw)
                        nw = o.mark(V.match_replace(wt[:, :], top[:, 8 * r:8 * r + 8], wt[:, :], 0.0))
                    if find_words and r == 3:
                        dve.wait_ge(order, nw)
                        nw = o.mark(V.tensor_copy(topi[:, :], top[:, 0:KEEP]))
                    if find_nodes:
                        dve.wait_ge(order, nn)
                        nn = o.mark(V.max(top2[:, 8 * r:8 * r + 8], work))
                if find_words:
                    dve.wait_ge(order, nw)
                    o.mark(V.tensor_scalar(hi[:, :], topi[:, :], 5, 0xFFFF8, ALU.logical_shift_right, ALU.bitwise_and))
                    o.mark(V.tensor_tensor(bt[:, :, :], topi[:, :].unsqueeze(2).to_broadcast([P, KEEP, WORD]),
                                           ci[:, :].unsqueeze(1).to_broadcast([P, KEEP, WORD]), ALU.bitwise_and))
                if find_nodes:
                    dve.wait_ge(order, nn)
                    V.tensor_scalar(idx[u][:, :], top2[:, 0:KEEP], -1.0, float(N), ALU.mult, ALU.add
                                    ).then_inc(S["idx_ready"], 1)

            def chunk_max(o, c, g, u=0):
                dve.wait_ge(gathered[c], (g + 1) * (16 * CHUNKS[c]))
                if c > 0:
                    dve.wait_ge(maxed[c - 1], g + 2)
                dst = gb[c + 1][:, 0, :] if c < 2 else hl[u][:, 1, :]
                if c == 2:
                    dve.wait_ge(S["cat_transposed"], g)
                V.tensor_reduce(dst, gb[c][:, :, :].rearrange("p k c -> p c k"), AX.X, ALU.max).then_inc(maxed[c], 1)

            o = Order(order)
            V.memset(zrow[:, :], 0.0)
            V.memset(ones[:, :], 1.0).then_inc(S["ones_ready"], 1)
            for c in range(3):
                dve.sem_inc(maxed[c], 1)
            dve.wait_ge(S["consts_in"], 16 * 6)
            o.mark(V.tensor_copy(cb[:, :], cf[:, 0:P + 16]))
            for k in range(2):
                n = o.mark(V.tensor_tensor(lk[:, 0:2 * C].rearrange("p (a o) -> p a o", a=2),
                                           w1[:, k, 0:C].unsqueeze(1).to_broadcast([P, 2, C]),
                                           val[0][:, 0:2 * C].rearrange("p (a o) -> p a o", a=2), ALU.mult))
                dve.wait_ge(order, n)
                n = o.mark(V.tensor_reduce(m_t[:, 0:2], lk[:, 0:2 * C].rearrange("p (a o) -> p a o", a=2), AX.X, ALU.add))
                dve.wait_ge(order, n)
                o.mark(V.tensor_copy(w1[:, k, C:C + 1], m_t[:, 1:2]))
                n = o.mark(V.tensor_copy(wa1[:, k, :], m_t[:, 0:1].to_broadcast([P, P])))
                dve.wait_ge(order, n)
            V.engine_nop().then_inc(S["weights_ready"], 1)
            for m in range(PAIRS):
                u = m % 2
                dve.wait_ge(xn_in[u], 16 * (m // 2 + 1))
                if m >= 2:
                    dve.wait_ge(S["hn_ready"], m - 1)
                dve.wait_ge(order, o.n)
                statistics(o, xn[u][:, 0, :], 0, u)
                statistics(o, xn[u][:, 1, :], 1, u, S["stats_ready"])
                if m >= 1:
                    normaliser(o, m - 1, 1 - u, slice(0, 2))
                if m in (2, 4, 6):
                    a = m // 2 - 1
                    read_words(o, a)
                    search(o, a, (a + 1) % 2, True, a > 0)
            normaliser(o, PAIRS - 1, 1, slice(0, 2))
            chunk_max(o, 0, 0)
            chunk_max(o, 1, 0)
            end_order(o)

            def item_value(o, i, j, jj, sweep):
                if not (type(i) is int and i < 2):
                    wait_apart(dve, "dve_passed", S["leaky_ready"], i - 1)
                wait_apart(dve, "dve_passed", S["blocked_ready"], i + 1)
                if sweep:
                    V.tensor_tensor(val[jj][:, 0:HALF], nbt[:, HALF:N], s1_all[:, HALF:N], ALU.add
                                    ).then_inc(S["val_ready"], 1)
                    return
                n = o.mark(V.tensor_tensor_reduce(out=val[jj][:, :], in0=nbt[:, :], in1=s1_all[:, :], scale=1.0,
                                                  scalar=-3e38, op0=ALU.add, op1=ALU.max, accum_out=m_t[:, 0:1]))
                dve.wait_ge(order, n)
                o.mark(V.tensor_scalar(m_t[:, 1:2], m_t[:, 0:1], SLOPE - 1, s2n[:, bass.ds(j, 1)], ALU.mult, ALU.add))
                n = o.mark(V.tensor_scalar(m_t[:, 2:3], m_t[:, 0:1], -SLOPE, None, ALU.mult))
                dve.wait_ge(order, n)
                V.scalar_tensor_tensor(out=nb[:, bass.ds(j, 1)], in0=m_t[:, 1:2], scalar=0.0, in1=m_t[:, 2:3],
                                       op0=ALU.min, op1=ALU.add).then_inc(S["val_ready"], 1)

            def item_leaky(o, i, jj, sweep, drain):
                w, q = HALF if sweep else N, lk_of(jj, drain)
                dve.wait_ge(S["relu_ready"], i + 1)
                V.scalar_tensor_tensor(out=q[:, 0:w], in0=val[jj][:, 0:w], scalar=SLOPE, in1=q[:, 0:w],
                                       op0=ALU.mult, op1=ALU.add).then_inc(S["leaky_ready"], 1)

            def item_rows(o, i, j, jj, sweep):
                if sweep == 0:
                    dve.wait_ge(S["exp_ready"], i + 1)
                    n = o.mark(V.tensor_tensor(zs[:, :], za[jj][:, 0:1], za[jj][:, 1:2], ALU.add))
                    dve.wait_ge(order, n)
                    n = o.mark(V.reciprocal(rz[:, bass.ds(j, 1)], zs[:, :]))
                    dve.wait_ge(order, n)
                dve.wait_ge(S["av_done"], i)
                V.tensor_scalar(hz[jj][:, :], h_all[:, bass.ds(j, 1), 0:C].rearrange("p a c -> p (a c)"),
                                rz[:, bass.ds(j, 1)], None, ALU.mult).then_inc(S["hz_ready"], 1)

            def flush(o, f):
                dve.wait_ge(S["gelu_done"], f + 1)
                dve.wait_ge(S["xo_in"], f * 16 + 16)
                dve.wait_ge(order, o.n)
                V.tensor_tensor(go[:, :, :], go[:, :, :], xo[:, :, :], ALU.add).then_inc(S["res_ready"], 1)

            def take_over(o, b):
                dve.wait_ge(S["h_saved"], b * TILES)
                o.mark(V.tensor_scalar(s2p[:, :], h_acc[:, :, C], 1 - SLOPE, None, ALU.mult))
                n = o.mark(V.tensor_scalar(s2n[:, :], h_acc[:, :, C], SLOPE - 1, None, ALU.mult))
                V.tensor_copy(s1_all[:, :], s1_acc[:, :]).then_inc(S["s1_copied"], 1)
                dve.wait_ge(order, n)
                wait_apart(dve, "dve_passed", S["s1_copied"], b)

            def step(o, b, i, u, t, n, words, nodes, l, g, new, old, fl, drain):
                v = b * TILES + i * 2 + u
                it = (b - 1) * 32 + i * 4 + u * 2
                sweep, before = t // 8 % 2, (t - 1) // 8 % 2
                j = i * 4 + u * 2 - 16 * sweep
                j1 = j - 1 if t % 8 else 15
                j2 = j - 2 if t % 8 else 14
                if words:
                    read_words(o, v + 3)
                if l:
                    chunk_max(o, 2, v, u)
                if new and t:
                    item_value(o, it, j, 0, sweep)
                if old:
                    item_rows(o, it - 2, j2, 0, before)
                if l:
                    dve.wait_ge(S["out0_done"], v + 1)
                    dve.wait_ge(l_in[u], (b * PAIRS + i) * 32 + 32)
                    dve.wait_ge(x1_stored[u], (b * PAIRS + i) * 16)
                    n1 = o.mark(V.scalar_tensor_tensor(out=x1[u][:, :], in0=ps_l[:, 0:C], scalar=0.0,
                                                       in1=xl[u][:, :], op0=ALU.max, op1=ALU.add))
                    if n:
                        m = (b + 1) * PAIRS + i * 2 + u
                        dve.wait_ge(xn_in[u], (b + 1) * 64 + i * 16 + 16)
                        dve.wait_ge(S["hn_ready"], m - 1)
                        n2 = o.mark(V.bn_stats(bn6[:, 0, :], xn[u][:, 0, :]))
                        n3 = o.mark(V.bn_stats(bn6[:, 1, :], xn[u][:, 1, :]))
                    dve.wait_ge(order, n1)
                    n1 = o.mark(V.bn_stats(bn6[:, 2, :], x1[u][:, :]))
                    if n:
                        dve.wait_ge(order, n3)
                        o.mark(V.bn_aggr(mv[u][:, 0, :], bn6[:, 0, :]))
                        o.mark(V.bn_aggr(mv[u][:, 1, :], bn6[:, 1, :]))
                    dve.wait_ge(order, n1)
                    V.bn_aggr(mv[u][:, 2, :], bn6[:, 2, :]).then_inc(S["stats_ready"], 1)
                if old:
                    item_leaky(o, it - 1, 1, before, drain)
                if new and not t:
                    take_over(o, b)
                    item_value(o, it, j, 0, sweep)
                if g:
                    chunk_max(o, 0, v + 1)
                if fl is not None:
                    flush(o, fl)
                if l:
                    normaliser(o, PAIRS + v, u, slice(0 if n else 2, 3))
                    dve.wait_ge(S["norm_ready"], PAIRS + v + 1)
                    V.tensor_scalar(y1[:, :], x1[u][:, :], rs[u][:, 2:3], nmr[u][:, 2:3], ALU.mult, ALU.add
                                    ).then_inc(S["y1_ready"], 1)
                if new:
                    item_value(o, it + 1, j + 1, 1, sweep)
                if old and not t:
                    item_rows(o, it - 1, j1, 1, before)
                if nodes:
                    search(o, v + 3, u, words, nodes)
                if new and not t:
                    dve.wait_ge(S["h_copied"], b)
                    o.mark(V.memset(zs[:, :], 0.0))
                if old and t:
                    item_rows(o, it - 1, j1, 1, before)
                if new:
                    item_leaky(o, it, 0, sweep, drain)
                if g:
                    chunk_max(o, 1, v + 1)

            def round_(b, first=False, last=False, drain=False):
                def pair(i, t0):
                    o = Order(order)
                    for u in range(2):
                        t = t0 + u
                        one = type(b) is int and b == 1
                        fl = {1: b * 2 - 3, 9: b * 2 - 2}.get(t) if not first and not (one and t == 1) else None
                        step(o, b, i, u, t, n=t < 8 and not last and not drain,
                             words=not drain and not (last and t >= 13), nodes=not drain and not (last and t >= 14),
                             l=not drain, g=not drain and not (last and t == 15),
                             new=not first, old=not first and not (one and t == 0), fl=fl, drain=drain)
                    end_order(o)
                for t0, i0, end in SECTIONS[last]:
                    if end == i0 + 1:
                        pair(i0, t0)
                    else:
                        with dve.Fori(i0, end) as i:
                            pair(i, t0)

            round_(0, first=True)
            round_(1)
            with dve.Fori(2, NB - 1) as b:
                round_(b)
            round_(NB - 1, last=True)
            round_(NB, drain=True)
            o = Order(order)
            step(o, NB + 1, 0, 0, 0, n=False, words=False, nodes=False, l=False, g=False, new=False, old=True,
                 fl=None, drain=True)
            flush(o, 2 * NB - 1)

        @block.tensor
        def _(pe):
            T = nc.tensor

            def transpose_signs(a):
                pe.wait_ge(S["signed"], a + 1)
                pe.wait_ge(S["edges_ready"], a)
                pe.wait_ge(S["words_read"], a)
                for m in range(TILES):
                    ins = T.transpose(sgt[:, m * P:(m + 1) * P], sg[:, m * P:(m + 1) * P], identb)
                ins.then_inc(S["signs_transposed"], 1)

            def make_words(a):
                pe.wait_ge(S["bits_ready"], a + 1)
                pe.wait_ge(S["edges_ready"], a + 1)
                for m in range(TILES):
                    ins = T.matmul(words[:, m * 16:(m + 1) * 16], bits[:, m, :], pack, start=True, stop=True)
                ins.then_inc(S["words_done"], 1)

            def av(i, jj):
                pe.wait_ge(S["exp_ready"], i + 1)
                pe.wait_ge(S["hz_ready"], i + 1)
                for k in range(8):
                    ins = T.matmul(ps_av[:, k * C:(k + 1) * C], ex[jj][:, k * P:(k + 1) * P], hz[jj][:, :],
                                   start=False, stop=False)
                ins.then_inc(S["av_done"], 1)

            def open_sweep(f):
                if not (type(f) is int and f == 0):
                    pe.wait_ge(S["gelu_done"], f)
                for k in range(4):
                    T.matmul(ps_av[:, k * 512:(k + 1) * 512], zeros[0:1, 0:P], zeros[0:1, :], start=True, stop=False)

            def close_sweep():
                for k in range(4):
                    ins = T.matmul(ps_av[:, k * 512:(k + 1) * 512], zeros[0:1, 0:P], zeros[0:1, :], start=False, stop=True)
                ins.then_inc(S["sweep_done"], 1)

            def step(b, i, u, t, a, l, old):
                v = b * TILES + i * 2 + u
                it = (b - 1) * 32 + i * 4 + u * 2
                if l:
                    pe.wait_ge(l_in[u], (b * PAIRS + i) * 32 + 32)
                    pe.wait_ge(maxed[2], v + 2)
                    for k in range(4):
                        ins = T.transpose(ps_t[:, k * P:(k + 1) * P], hl[u][:, k // 2, k % 2 * P:(k % 2 + 1) * P], ident)
                    ins.then_inc(S["cat_transposed"], 1)
                    pe.wait_ge(S["cat_ready"], v + 1)
                    pe.wait_ge(S["h_saved"], v)
                    for k in range(4):
                        T.matmul(ps_l[:, 0:C], hcat[:, k, :], w0[:, k, :], start=k == 0, stop=False)
                    T.matmul(ps_l[:, 0:C], ones[:, :], bias0[:, :], start=False, stop=True).then_inc(S["out0_done"], 1)
                if old and t % 8 == 1:
                    open_sweep(b * 2 - 2 + t // 8)
                if old:
                    av(it - 2, 0)
                if a:
                    transpose_signs(v + 4)
                if l:
                    pe.wait_ge(S["y1_ready"], v + 1)
                    for k in range(2):
                        ins = T.transpose(ps_t[:, k * P:(k + 1) * P], y1[:, k * P:(k + 1) * P], ident)
                    ins.then_inc(S["y1_transposed"], 1)
                if a:
                    make_words(v + 4)
                if l:
                    pe.wait_ge(S["h1t_ready"], v + 1)
                    for k in range(2):
                        T.matmul(ps_l[:, 0:C + 1], h1t[:, k, :], w1[:, k, :], start=k == 0, stop=k == 1)
                    for k in range(2):
                        ins = T.matmul(ps_l[:, 384:384 + P], wa1[:, k, :], h1t[:, k, :], start=k == 0, stop=k == 1)
                    ins.then_inc(S["h_done"], 1)
                if old:
                    av(it - 1, 1)
                    if t % 8 == 0:
                        close_sweep()

            pe.sem_inc(S["av_done"], 1)
            pe.wait_ge(S["consts_in"], 16 * 6)
            pe.wait_ge(S["ones_ready"], 3)
            pe.wait_ge(S["weights_ready"], 1)
            for a in range(4):
                transpose_signs(a)
                make_words(a)

            def round_(b, first=False, last=False, drain=False):
                def pair(i, t0):
                    for u in range(2):
                        t = t0 + u
                        step(b, i, u, t, a=not drain and not (last and t >= 12), l=not drain,
                             old=not first and not (type(b) is int and b == 1 and t == 0))
                for t0, i0, end in SECTIONS[last]:
                    if end == i0 + 1:
                        pair(i0, t0)
                    else:
                        with pe.Fori(i0, end) as i:
                            pair(i, t0)

            round_(0, first=True)
            round_(1)
            with pe.Fori(2, NB - 1) as b:
                round_(b)
            round_(NB - 1, last=True)
            round_(NB, drain=True)
            step(NB + 1, 0, 0, 0, a=False, l=False, old=True)


def constants():
    import numpy as np
    f = np.zeros((P, C_COLS), np.float32)
    f[:, C_ID:C_ID + P] = np.eye(P)
    f[:, C_KEY:C_KEY + WORDS] = (WORDS - np.arange(WORDS)) * (1 << WORD)
    f[:, C_IOTA:C_IOTA + WORD] = np.arange(WORD)
    for m in range(P):
        f[m, C_PACK + m // WORD] = 2.0 ** (WORD - 1 - m % WORD)
    i = np.zeros((P, WORD), np.int32)
    i[:, :] = 1 << (WORD - 1 - np.arange(WORD))
    return {"const_f": f, "const_i": i}


def kernel(x, adj, L0_gnn_W, L0_gnn_b, L1_gnn_W, L1_gnn_a):
    import numpy as np
    import concourse.bacc as bacc
    from concourse.bass_utils import run_bass_kernel_spmd

    nc = bacc.Bacc("TRN2", target_bir_lowering=False, num_devices=1)
    given = {"x": x, "adj": adj, "L0_gnn_W": L0_gnn_W, "L0_gnn_b": L0_gnn_b, "L1_gnn_W": L1_gnn_W,
             "L1_gnn_a": L1_gnn_a, **constants()}
    arrays = {f"in_{k}": np.ascontiguousarray(v) for k, v in given.items()}
    args = [nc.dram_tensor(k, a.shape, mybir.dt.from_np(a.dtype), kind="ExternalInput").ap() for k, a in arrays.items()]
    out = nc.dram_tensor("out_0", (NB, N, C), fp32, kind="ExternalOutput").ap()
    graph_layers(nc, *args, out)
    return run_bass_kernel_spmd(nc, [arrays], core_ids=[0]).results[0]["out_0"]
```

```python
from contextlib import ExitStack

import concourse.bass as bass
from concourse import mybir

fp32 = mybir.dt.float32
bf16 = mybir.dt.bfloat16
i32 = mybir.dt.int32
u8 = mybir.dt.uint8
ALU = mybir.AluOpType
ACT = mybir.ActivationFunctionType
AX = mybir.AxisListType

P = 128
NB, N, C = 8, 2048, 256
TILES = N // P
HALF = N // 2
KEEP = 25
ROWS = N + 1
WORD = 8
WORDS = N // WORD
CHUNKS = (13, 12)
PAIRS = TILES // 2
N_FIRST = 6
EPS = 1e-5
EXP_AND_LN = 6
SLOPE = 0.4
BLOCKED = 1e30

C_ID, C_IOTA = 0, P
C_PACK = C_IOTA + WORD
C_ONE = C_PACK + 16
C_KEY = C_ONE + P
C_COLS = C_KEY + WORDS


class Order:

    def __init__(self, sem):
        self.sem, self.n = sem, 0

    def mark(self, instruction):
        instruction.then_inc(self.sem, 1)
        self.n += 1
        return self.n


def graph_layers(nc, x, adj, W0, b0, W1, a1, const_f, const_i, out):
    ctx = ExitStack()
    with ctx:
        def sb(name, shape, dt):
            return ctx.enter_context(nc.sbuf_tensor(name, shape, dt))

        def ps(name, shape, dt):
            return ctx.enter_context(nc.psum_tensor(name, shape, dt))

        def sem(name):
            return ctx.enter_context(nc.semaphore(name))

        table = [nc.dram_tensor(f"h_table{u}", (ROWS, C), fp32).ap() for u in range(2)]
        edges_t = nc.dram_tensor("edges_t", (NB * N, N), u8).ap()
        x1_dram = nc.dram_tensor("x1_rows", (NB * N, C), fp32).ap()
        x_rows = x.rearrange("b n c -> (b n) c")
        adj_rows = adj.rearrange("b n m -> (b n) m")
        out_rows = out.rearrange("b n c -> (b n) c")

        cf = sb("cf", [P, C_PACK], fp32)
        cb = sb("cb", [P, C_COLS], bf16)
        ci = sb("ci", [P, WORD], i32)
        ident, identb, pack = cf[:, C_ID:C_ID + P], cb[:, C_ID:C_ID + P], cb[:, C_PACK:C_PACK + 16]
        one_row, key_row = cb[0:1, C_ONE:C_ONE + P], cb[0:1, C_KEY:C_KEY + WORDS]
        w0 = sb("w0", [P, 4, C], fp32)
        w1 = sb("w1", [P, 2, C + 1], fp32)
        wa1 = sb("wa1", [P, 2, P], fp32)
        bias0 = sb("bias0", [1, C], fp32)
        ones = sb("ones", [1, P], fp32)
        zeros = sb("zeros", [1, 512], bf16)
        zrow = sb("zrow", [1, C], fp32)

        xn = [sb(f"xn{u}", [P, 2, C], fp32) for u in range(2)]
        bn6 = sb("bn6", [P, 3, 6], fp32)
        mv = [sb(f"mv{u}", [P, 3, 2], fp32) for u in range(2)]
        lnv = [sb(f"lnv{u}", [P, 3], fp32) for u in range(2)]
        rs0 = [sb(f"rs0_{u}", [P, 3], fp32) for u in range(2)]
        rs = [sb(f"rs{u}", [P, 3], fp32) for u in range(2)]
        nmr = [sb(f"nmr{u}", [P, 3], fp32) for u in range(2)]
        lt = sb("lt", [P, 2, 3], fp32)
        ad = [sb(f"ad{u}", [P, N], i32) for u in range(2)]
        sg = sb("sg", [P, N], bf16)
        bits = sg[:, :].rearrange("p (m n) -> p m n", n=P)
        stage = sb("stage", [P, TILES, 8 * P], u8)
        wb = sb("wb", [P, WORDS], fp32)
        wv = sb("wv", [P, WORDS], fp32)
        wt = sb("wt", [P, WORDS], fp32)
        top = sb("top", [P, 32], fp32)
        topi = sb("topi", [P, KEEP], i32)
        hi = sb("hi", [P, KEEP], i32)
        bt = sb("bt", [P, KEEP, WORD], i32)
        cand = sb("cand", [P, KEEP, WORD], fp32)
        cand2 = sb("cand2", [P, KEEP, WORD], fp32)
        top2 = sb("top2", [P, 32], fp32)
        idx = [sb(f"idx{u}", [P, KEEP], i32) for u in range(2)]
        gb = [sb(f"gb{c}", [P, n + (c > 0), C], fp32) for c, n in enumerate(CHUNKS)]
        xl = [sb(f"xl{u}", [P, C], fp32) for u in range(2)]
        hl = [sb(f"hl{u}", [P, 2, C], fp32) for u in range(2)]
        hcat = sb("hcat", [P, 4, P], fp32)
        x1 = [sb(f"x1_{u}", [P, C], fp32) for u in range(2)]
        y1 = sb("y1", [P, C], fp32)
        h1t = sb("h1t", [P, 2, P], fp32)
        h_acc = sb("h_acc", [P, TILES, C + 1], fp32)
        s1_acc = sb("s1_acc", [P, N], fp32)
        h_all = sb("h_all", [P, TILES, C + 1], fp32)
        s1_all = sb("s1_all", [P, N], fp32)
        s2p = sb("s2p", [P, TILES], fp32)
        s2n = sb("s2n", [P, TILES], fp32)
        edge = [sb(f"edge{u}", [P, 2, N], u8) for u in range(2)]
        nbt = sb("nbt", [P, N], bf16)
        val = [sb(f"val{u}", [P, N], fp32) for u in range(2)]
        lk = [sb(f"lk{u}", [P, N], fp32) for u in range(2)]
        hz = [sb(f"hz{u}", [P, C], fp32) for u in range(2)]
        m_t = sb("m_t", [P, 2], fp32)
        m_a = sb("m_a", [P, 2, 2], fp32)
        nb = sb("nb", [P, TILES], fp32)
        za = sb("za", [P, TILES], fp32)
        rz = sb("rz", [P, TILES], fp32)
        xo = sb("xo", [P, 8, C], fp32)
        go = sb("go", [P, 8, C], fp32)

        ps_av = ps("ps_av", [P, 8 * C], fp32)
        ps_c = ps("ps_c", [P, 1024], fp32)
        ps_t = ps("ps_t", [P, 512], fp32)
        ps_l = ps("ps_l", [P, 512], fp32)
        sgt = ps_c[:, :].bitcast(bf16)
        words, keyed = ps_c[:, 0:WORDS], ps_c[:, WORDS:2 * WORDS]

        S = {n: sem(n) for n in (
            "consts_in", "weights_in", "bf16_ready", "weights_ready", "ones_ready", "zeros_ready", "zrow_stored",
            "signed", "signs_transposed", "bits_ready", "edges_ready", "edges_stored", "words_done", "words_scaled", "words_read",
            "idx_ready", "stats_ready", "ln_ready", "rs0_ready", "norm_ready", "hn_ready",
            "agg_ready", "cat_transposed", "cat_ready", "out0_done", "y1_ready", "y1_transposed", "h1t_ready",
            "h_done", "h_saved", "h_copied", "s_copied",
            "blocked_ready", "val_ready", "relu_ready", "leaky_ready", "exp_ready", "hz_ready", "av_done",
            "sweep_done", "gelu_done", "xo_in", "res_ready", "out_stored", "order",
            "sp_passed", "pool_passed", "dve_passed")}
        adj_in = [sem(f"adj_in{u}") for u in range(2)]
        first_in = [sem(f"first_in{m}") for m in range(PAIRS)]
        xn_in = [sem(f"xn_in{u}") for u in range(2)]
        hn_stored = [sem(f"hn_stored{u}") for u in range(2)]
        l_in = [sem(f"l_in{u}") for u in range(2)]
        x1_stored = [sem(f"x1_stored{u}") for u in range(2)]
        edge_in = [sem(f"edge_in{u}") for u in range(2)]
        gathered = [sem(f"gathered{c}") for c in range(len(CHUNKS))]
        maxed = [sem(f"maxed{c}") for c in range(len(CHUNKS))]

        def blocked_of(jj, drain):
            return gb[0][:, 8:12, :].rearrange("p k c -> p (k c)").bitcast(bf16) if drain and jj else nbt

        def lk_of(jj, u, drain):
            return gb[jj][:, 0:8, :].rearrange("p k c -> p (k c)") if drain and u == 0 else lk[jj]

        SECTIONS = {False: [(0, 0, 1), (2, 1, 3), (6, 3, 4), (8, 4, 5), (10, 5, 7), (14, 7, 8)],
                    True: [(0, 0, 1), (2, 1, 4), (8, 4, 5), (10, 5, 6), (12, 6, 7), (14, 7, 8)]}

        def wait_apart(engine, name, semaphore, value):
            engine.wait_ge(semaphore, value)
            engine.sem_inc(S[name], 1)

        def first_rows(m):
            return h_all[:, 2 * m:2 * m + 2, 0:C]

        block = ctx.enter_context(nc.Block())

        @block.sync
        def _(sp):
            def load_adj(a, u):
                sp.dma_start(ad[u][:, :], adj_rows[bass.ds(a * P, P), :]).then_inc(adj_in[u], 16)

            def load_xn(m, dst, loaded):
                sp.dma_start(dst, x_rows[bass.ds(m * 2 * P, 2 * P), :].rearrange("(k p) c -> p k c", p=P)
                             ).then_inc(loaded, 16)

            def store_hn(tb, k, m, u, src):
                wait_apart(sp, "sp_passed", S["hn_ready"], m + 1)
                sp.dma_start(table[tb][k * 2 * P:(k + 1) * 2 * P, :].rearrange("(k p) c -> p k c", p=P), src
                             ).then_inc(hn_stored[u], 16)

            def load_l(tb, b, t, u):
                sp.dma_start(xl[u][:, :], x_rows[bass.ds(b * N + t * P, P), :]).then_inc(l_in[u], 16)
                sp.dma_start(hl[u][:, 0, :], table[tb][t * P:(t + 1) * P, :]).then_inc(l_in[u], 16)

            def load_edge(bt_, t, u):
                sp.dma_start(edge[u][:, :, :], edges_t[bass.ds(bt_ * N + (t % 8) * 2 * P, 2 * P), :]
                             .rearrange("(k p) n -> p k n", p=P)).then_inc(edge_in[u], 16)

            sp.dma_start(cf[:, :], const_f[:, 0:C_PACK]).then_inc(S["consts_in"], 16)
            sp.dma_start(val[1][:, 0:C_COLS], const_f).then_inc(S["consts_in"], 16)
            sp.dma_start(ci[:, :], const_i).then_inc(S["consts_in"], 16)
            load_adj(0, 0)
            for m in range(PAIRS):
                load_xn(m, first_rows(m), first_in[m])
            load_adj(1, 1)
            sp.dma_start(w0[:, :, :], W0.rearrange("(k p) o -> p k o", p=P)).then_inc(S["weights_in"], 16)
            sp.dma_start(w1[:, :, 0:C], W1.rearrange("(k p) o -> p k o", p=P)).then_inc(S["weights_in"], 16)
            sp.dma_start(bias0[:, :], b0.rearrange("(a o) -> a o", a=1)).then_inc(S["weights_in"], 16)
            sp.dma_start(val[0][:, 0:2 * C], a1.rearrange("f a -> a f").to_broadcast([P, 2 * C])).then_inc(S["weights_in"], 16)
            sp.sem_inc(S["edges_stored"], 16)
            wait_apart(sp, "sp_passed", S["ones_ready"], 1)
            for tb in range(2):
                sp.dma_start(table[tb][N:ROWS, :], zrow[:, :]).then_inc(S["zrow_stored"], 16)
            for m in range(PAIRS):
                store_hn(0, m, m, m % 2, first_rows(m))
            for a in range(4):
                wait_apart(sp, "sp_passed", S["signed"], a + 1)
                load_adj(2 + a, a % 2)
            for u in range(2):
                wait_apart(sp, "sp_passed", hn_stored[u], 16 * PAIRS // 2)
            load_l(0, 0, 0, 0)

            def store_edges(b, q):
                g4 = b * 4 + q
                wait_apart(sp, "sp_passed", S["edges_ready"], g4 * 4 + 4)
                wait_apart(sp, "sp_passed", S["edges_stored"], g4 * 16 + 16)
                at = 4 * P * (q % 2)
                sp.dma_start(edges_t.rearrange("(b m p) n -> b p m n", p=P, m=TILES)[bass.ds(b, 1)]
                             .rearrange("b p m n -> p (b m) n")[:, :, q * 4 * P:(q + 1) * 4 * P],
                             stage[:, :, at:at + 4 * P]).then_inc(S["edges_stored"], 16)

            store_edges(0, 0)

            def step(b, tb, t, n, a, l, e, w, last):
                v = b * TILES + t
                u = t % 2
                if n:
                    m = (b + 1) * PAIRS + t - N_FIRST
                    wait_apart(sp, "sp_passed", hn_stored[u], (b + 1) * 64 + (t - N_FIRST) // 2 * 16)
                    load_xn(m, xn[u][:, :, :], xn_in[u])
                if e:
                    nt = (t + 1) % 16
                    eb = b - 1 + (t + 1) // 16
                    if t == 15:
                        wait_apart(sp, "sp_passed", S["edges_stored"], 16 * 4 * eb + 16 * 5)
                    if w:
                        wait_apart(sp, "sp_passed", S["blocked_ready"], (b - 1) * 32 + 2 * t)
                    load_edge(eb, nt, nt % 2)
                if l and not (type(b) is int and b == NB - 1 and t == 15):
                    wait_apart(sp, "sp_passed", S["cat_transposed"], v)
                    wait_apart(sp, "sp_passed", S["stats_ready"], PAIRS + v)
                    if t == 15:
                        for k in range(2):
                            wait_apart(sp, "sp_passed", hn_stored[k], b * 64 + 128)
                        load_l(1 - tb, b + 1, 0, 0)
                    else:
                        load_l(tb, b, t + 1, (t + 1) % 2)
                if a:
                    wait_apart(sp, "sp_passed", S["signed"], v + 5)
                    load_adj(v + 6, u)
                if l:
                    wait_apart(sp, "sp_passed", S["stats_ready"], PAIRS + v + 1)
                    sp.dma_start(x1_dram[bass.ds(v * P, P), :], x1[u][:, :]).then_inc(x1_stored[u], 16)
                if n:
                    if t == N_FIRST:
                        wait_apart(sp, "sp_passed", maxed[1], b * TILES + 1)
                        wait_apart(sp, "sp_passed", S["cat_transposed"], b * TILES)
                    store_hn(1 - tb, t - N_FIRST, m, u, xn[u][:, :, :])
                if t % 4 == 3 and l and not (last and t == 15):
                    store_edges(b + (t + 1) // 16, (t + 1) // 4 % 4)

            def load_xo(bt_, h, f):
                wait_apart(sp, "sp_passed", S["res_ready"], f)
                for u in range(2):
                    wait_apart(sp, "sp_passed", x1_stored[u], bt_ * 128 + 128)
                sp.dma_start(xo[:, :, :], x1_dram[bass.ds(bt_ * N + h * HALF, HALF), :]
                             .rearrange("(k p) c -> p k c", p=P)).then_inc(S["xo_in"], 16)

            def store_out(bt_, h, f):
                wait_apart(sp, "sp_passed", S["res_ready"], f + 1)
                sp.dma_start(out_rows[bass.ds(bt_ * N + h * HALF, HALF), :].rearrange("(k p) c -> p k c", p=P),
                             go[:, :, :]).then_inc(S["out_stored"], 16)

            def round_(b, tb, first=False, last=False, drain=False):
                for t in range(TILES):
                    step(b, tb, t, n=0 <= t - N_FIRST < PAIRS and not last and not drain, a=not drain and not (last and t >= 10),
                         l=not drain, e=(not first or t == 15) and not (drain and t == 15),
                         w=not first and not (type(b) is int and b == 1 and t == 0), last=last)
                    if not first:
                        if t == 1 and not (type(b) is int and b == 1):
                            store_out(b - 2, 1, b * 2 - 3)
                        if t == 4:
                            load_xo(b - 1, 0, b * 2 - 2)
                        if t == 9:
                            store_out(b - 1, 0, b * 2 - 2)
                        if t == 12:
                            load_xo(b - 1, 1, b * 2 - 1)

            round_(0, 0, first=True)
            round_(1, 1)
            with sp.Fori(2, NB - 2, 2) as b:
                round_(b, 0)
                round_(b + 1, 1)
            round_(NB - 2, 0)
            round_(NB - 1, 1, last=True)
            round_(NB, 0, drain=True)
            store_out(NB - 1, 1, 2 * NB - 1)
            wait_apart(sp, "sp_passed", S["out_stored"], 16 * 2 * NB)

        @block.gpsimd
        def _(pool):
            nc.gpsimd.memset(zeros[:, :], 0.0).then_inc(S["zeros_ready"], 1)
            pool.wait_ge(S["zrow_stored"], 32)
            with pool.Fori(0, NB, 2) as b2:
                for tb in range(2):
                    b = b2 + tb
                    for u in range(2):
                        wait_apart(pool, "pool_passed", hn_stored[u], b * 64 + 64)
                    with pool.Fori(0, PAIRS) as i:
                        for u in range(2):
                            g = b * TILES + i * 2 + u
                            wait_apart(pool, "pool_passed", S["idx_ready"], g + 1)
                            k = 0
                            for c, n in enumerate(CHUNKS):
                                wait_apart(pool, "pool_passed", maxed[c], g + 1)
                                for s in range(n):
                                    pool.indirect_dma_start(gb[c][:, s + (c > 0), :], None, table[tb],
                                                            bass.IndirectOffsetOnAxis(idx[u][:, k:k + 1], 0)
                                                            ).then_inc(gathered[c], 16)
                                    k += 1

        @block.scalar
        def _(act):

            def sign(k, a, u):
                act.wait_ge(adj_in[u], k * 16 + 16)
                act.wait_ge(S["words_done"], a)
                nc.scalar.activation(sg[:, :], ad[u][:, :], ACT.Sign).then_inc(S["signed"], 1)

            def evacuate_signs(a, col):
                act.wait_ge(S["signs_transposed"], a + 1)
                nc.scalar.activation(bits, sgt.rearrange("p (m n) -> p m n", n=P), ACT.Square).then_inc(S["bits_ready"], 1)
                act.wait_ge(S["edges_stored"], a // 4 * 16)
                nc.scalar.activation(stage[:, :, bass.ds(col, P)], sgt.rearrange("p (m n) -> p m n", n=P), ACT.Relu
                                     ).then_inc(S["edges_ready"], 1)

            def scale_words(a):
                act.wait_ge(S["words_done"], a + 1)
                nc.scalar.activation(wb[:, :], words, ACT.Identity, scale=float(1 << 20)).then_inc(S["words_scaled"], 1)

            def root(q, u, cols):
                act.wait_ge(S["stats_ready"], q + 1)
                nc.scalar.activation(lnv[u][:, cols], mv[u][:, cols, 1], ACT.Ln, bias=EPS).then_inc(S["ln_ready"], 1)
                act.wait_ge(S["ln_ready"], q + 1)
                nc.scalar.activation(rs0[u][:, cols], lnv[u][:, cols], ACT.Exp, scale=-0.5).then_inc(S["rs0_ready"], 1)

            def norm_pair(q, u, rows):
                act.wait_ge(S["norm_ready"], q + 1)
                for k in range(2):
                    ins = nc.scalar.activation(rows[:, k, :], rows[:, k, :], ACT.Relu,
                                               bias=nmr[u][:, k:k + 1], scale=rs[u][:, k:k + 1])
                ins.then_inc(S["hn_ready"], 1)

            def load_tables():
                act.add_instruction(mybir.InstLoadActFuncSet(
                    name=nc.get_next_instruction_name(), engine=mybir.EngineType.Activation,
                    act_func_set_id=EXP_AND_LN, ins=[], outs=[]))

            def first_masks(a):
                sign(a // 2, a, a % 2)
                evacuate_signs(a, a * P)
                scale_words(a)

            load_tables()
            first_masks(0)
            for m in range(PAIRS):
                u = m % 2
                act.wait_ge(first_in[m], 16)
                root(m, u, slice(0, 2))
                norm_pair(m, u, first_rows(m))
            for a in range(1, 4):
                first_masks(a)

            def blocked(i, k, jj, u, cols, drain):
                act.wait_ge(edge_in[u], k * 16 + 16)
                act.wait_ge(S["val_ready"], i - drain)
                nc.scalar.activation(blocked_of(jj, drain)[:, cols], edge[u][:, jj, cols], ACT.Identity, scale=BLOCKED, bias=-BLOCKED
                                     ).then_inc(S["blocked_ready"], 1)

            def relu_part(i, j, jj, sweep, u, drain):
                w = HALF if sweep else N
                act.wait_ge(S["val_ready"], i + 1)
                act.wait_ge(S["av_done"], i - 2 if drain else i)
                nc.scalar.activation(lk_of(jj, u, drain)[:, 0:w], val[jj][:, 0:w], ACT.Relu, scale=1 - SLOPE,
                                     bias=s2p[:, bass.ds(j, 1)]).then_inc(S["relu_ready"], 1)

            def exp_part(i, j, jj, sweep, u, drain):
                act.wait_ge(S["leaky_ready"], i + 1)
                bias, q = nb[:, bass.ds(j, 1)], lk_of(jj, u, drain)
                if sweep == 0:
                    nc.scalar.activation(q[:, :], q[:, :], ACT.Exp, bias=bias, accum_out=za[:, bass.ds(j, 1)]
                                         ).then_inc(S["exp_ready"], 1)
                else:
                    nc.scalar.activation(q[:, 0:HALF], q[:, 0:HALF], ACT.Exp, bias=bias).then_inc(S["exp_ready"], 1)

            def flush(f):
                act.wait_ge(S["sweep_done"], f + 1)
                act.wait_ge(S["out_stored"], f * 16)
                nc.scalar.activation(go[:, :, :], ps_av[:, :].rearrange("p (k c) -> p k c", c=C), ACT.Gelu
                                     ).then_inc(S["gelu_done"], 1)
                load_tables()

            def step(b, i, u, t, n, a, l, new, old, fl, drain):
                v = b * TILES + i * 2 + u
                k = b * PAIRS + i
                it = (b - 1) * 32 + i * 4 + u * 2
                sweep, before = t // 8 % 2, (t - 1) // 8 % 2
                j = i * 4 + u * 2 - 16 * sweep
                j1 = j - 1 if t % 8 else 15
                j2 = j - 2 if t % 8 else 14
                cols = slice(HALF, N) if sweep else slice(0, N)
                if new:
                    blocked(it, k - PAIRS, 0, u, cols, drain and t > 0)
                if old and not drain:
                    exp_part(it - 2, j2, 0, before, 1 - u, drain)
                if old:
                    relu_part(it - 1, j1, 1, before, 1 - u, drain and t > 0)
                if old and drain:
                    exp_part(it - 2, j2, 0, before, 1 - u, drain)
                if l:
                    act.wait_ge(S["cat_transposed"], v + 1)
                    nc.scalar.copy(hcat[:, :, :], ps_t[:, :].rearrange("p (k n) -> p k n", n=P)).then_inc(S["cat_ready"], 1)
                if fl is not None:
                    flush(fl)
                if new:
                    blocked(it + 1, k - PAIRS, 1, u, cols, drain)
                if a:
                    sign(k + 2, v + 4, u)
                if l:
                    root(PAIRS + v, u, slice(0 if n else 2, 3))
                if a:
                    evacuate_signs(v + 4, (v + 4) % 8 * P)
                if l:
                    act.wait_ge(S["norm_ready"], PAIRS + v + 1)
                    nc.scalar.activation(y1[:, :], x1[u][:, :], ACT.Relu, bias=nmr[u][:, 2:3], scale=rs[u][:, 2:3]
                                         ).then_inc(S["y1_ready"], 1)
                if old and not (drain and new):
                    exp_part(it - 1, j1, 1, before, 1 - u, drain)
                if l:
                    act.wait_ge(S["y1_transposed"], v + 1)
                    nc.scalar.copy(h1t[:, :, :], ps_t[:, 0:C].rearrange("p (k n) -> p k n", n=P)
                                   ).then_inc(S["h1t_ready"], 1)
                if new:
                    if not t:
                        act.wait_ge(S["s_copied"], b)
                    relu_part(it, j, 0, sweep, u, drain)
                if old and drain and new:
                    exp_part(it - 1, j1, 1, before, 1 - u, drain)
                if t == 0 and new:
                    act.wait_ge(S["h_saved"], b * TILES)
                    act.wait_ge(S["hz_ready"], (b - 1) * 32)
                    nc.scalar.copy(h_all[:, :, :], h_acc[:, :, :]).then_inc(S["h_copied"], 1)
                if l:
                    act.wait_ge(S["h_done"], v + 1)
                    if not (type(b) is int and b == 0):
                        act.wait_ge(S["s_copied"], b)
                        act.wait_ge(S["h_copied"], b)
                    nc.scalar.copy(h_acc[:, bass.ds(i * 2 + u, 1), :].rearrange("p a c -> p (a c)"), ps_l[:, 0:C + 1])
                    nc.scalar.copy(s1_acc[:, bass.ds((i * 2 + u) * P, P)], ps_l[:, 384:384 + P]).then_inc(S["h_saved"], 1)
                if a:
                    scale_words(v + 4)
                if n:
                    norm_pair(PAIRS + v, u, xn[u])

            def round_(b, first=False, last=False, drain=False):
                def pair(i, t0):
                    for u in range(2):
                        t = t0 + u
                        one = type(b) is int and b == 1
                        fl = {1: b * 2 - 3, 9: b * 2 - 2}.get(t) if not first and not (one and t == 1) else None
                        step(b, i, u, t, n=0 <= t - N_FIRST < PAIRS and not last and not drain, a=not drain and not (last and t >= 12),
                             l=not drain, new=not first, old=not first and not (one and t == 0), fl=fl, drain=drain)
                for t0, i0, end in SECTIONS[last]:
                    if end == i0 + 1:
                        pair(i0, t0)
                    else:
                        with act.Fori(i0, end) as i:
                            pair(i, t0)

            round_(0, first=True)
            round_(1)
            with act.Fori(2, NB - 1) as b:
                round_(b)
            round_(NB - 1, last=True)
            round_(NB, drain=True)
            step(NB + 1, 0, 0, 0, n=False, a=False, l=False, new=False, old=True, fl=None, drain=True)
            flush(2 * NB - 1)

        @block.vector
        def _(dve):
            order = S["order"]
            V = nc.vector

            def end_order(o):
                dve.wait_ge(order, o.n)
                dve.sem_clear(order)

            def statistics(o, src, slot, u, ready=None):
                n = o.mark(V.bn_stats(bn6[:, slot, :], src))
                dve.wait_ge(order, n)
                ins = V.bn_aggr(mv[u][:, slot, :], bn6[:, slot, :])
                if ready is not None:
                    ins.then_inc(ready, 1)
                else:
                    o.mark(ins)

            def normaliser(o, q, u, cols):
                mean, var = mv[u][:, cols, 0], mv[u][:, cols, 1]
                dve.wait_ge(S["rs0_ready"], q + 1)
                dve.wait_ge(order, o.n)
                n = o.mark(V.tensor_tensor(lt[:, 0, cols], rs0[u][:, cols], rs0[u][:, cols], ALU.mult))
                dve.wait_ge(order, n)
                n = o.mark(V.scalar_tensor_tensor(out=lt[:, 1, cols], in0=var, scalar=EPS, in1=lt[:, 0, cols],
                                                  op0=ALU.add, op1=ALU.mult))
                dve.wait_ge(order, n)
                n = o.mark(V.tensor_scalar(lt[:, 0, cols], lt[:, 1, cols], -0.5, 1.5, ALU.mult, ALU.add))
                dve.wait_ge(order, n)
                n = o.mark(V.tensor_tensor(rs[u][:, cols], rs0[u][:, cols], lt[:, 0, cols], ALU.mult))
                dve.wait_ge(order, n)
                V.scalar_tensor_tensor(out=nmr[u][:, cols], in0=mean, scalar=-1.0, in1=rs[u][:, cols],
                                       op0=ALU.mult, op1=ALU.mult).then_inc(S["norm_ready"], 1)

            def read_words(o, a):
                dve.wait_ge(S["words_scaled"], a + 1)
                V.tensor_tensor(wv[:, :], keyed, wb[:, :], ALU.min).then_inc(S["words_read"], 1)

            def search(o, a, u, find_words, find_nodes):
                nodes = cand[:, :, :].rearrange("p k w -> p (k w)")
                work = cand2[:, :, :].rearrange("p k w -> p (k w)")
                nw = nn = o.n
                if find_words:
                    wait_apart(dve, "dve_passed", S["words_read"], a + 1)
                if find_nodes:
                    dve.wait_ge(order, nn)
                    nn = o.mark(V.tensor_tensor(cand2[:, :, :], hi[:, :].unsqueeze(2).to_broadcast([P, KEEP, WORD]),
                                                cf[:, C_IOTA:C_IOTA + WORD].unsqueeze(1).to_broadcast([P, KEEP, WORD]),
                                                ALU.subtract))
                if find_words:
                    dve.wait_ge(order, nw)
                    nw = o.mark(V.max(top[:, 0:8], wv[:, :]))
                if find_nodes:
                    dve.wait_ge(order, nn)
                    nn = o.mark(V.scalar_tensor_tensor(out=cand[:, :, :], in0=bt[:, :, :], scalar=0.0,
                                                       in1=cand2[:, :, :], op0=ALU.is_gt, op1=ALU.mult))
                if find_words:
                    dve.wait_ge(order, nw)
                    nw = o.mark(V.match_replace(wt[:, :], top[:, 0:8], wv[:, :], 0.0))
                if find_nodes:
                    dve.wait_ge(order, nn)
                    nn = o.mark(V.max(top2[:, 0:8], nodes))
                for r in range(1, 4):
                    if find_words:
                        dve.wait_ge(order, nw)
                        nw = o.mark(V.max(top[:, 8 * r:8 * r + 8], wt[:, :]))
                    if find_nodes:
                        dve.wait_ge(order, nn)
                        nn = o.mark(V.match_replace(work, top2[:, 8 * r - 8:8 * r], nodes if r == 1 else work, 0.0))
                    if find_words and r < 3:
                        dve.wait_ge(order, nw)
                        nw = o.mark(V.match_replace(wt[:, :], top[:, 8 * r:8 * r + 8], wt[:, :], 0.0))
                    if find_words and r == 3:
                        dve.wait_ge(order, nw)
                        nw = o.mark(V.tensor_copy(topi[:, :], top[:, 0:KEEP]))
                    if find_nodes:
                        dve.wait_ge(order, nn)
                        nn = o.mark(V.max(top2[:, 8 * r:8 * r + 8], work))
                if find_words:
                    dve.wait_ge(order, nw)
                    o.mark(V.tensor_scalar(hi[:, :], topi[:, :], 5, 0xFFFF8, ALU.logical_shift_right, ALU.bitwise_and))
                    o.mark(V.tensor_tensor(bt[:, :, :], topi[:, :].unsqueeze(2).to_broadcast([P, KEEP, WORD]),
                                           ci[:, :].unsqueeze(1).to_broadcast([P, KEEP, WORD]), ALU.bitwise_and))
                if find_nodes:
                    dve.wait_ge(order, nn)
                    V.tensor_scalar(idx[u][:, :], top2[:, 0:KEEP], -1.0, float(N), ALU.mult, ALU.add
                                    ).then_inc(S["idx_ready"], 1)

            def chunk_max(o, c, g, u=0):
                dve.wait_ge(gathered[c], (g + 1) * (16 * CHUNKS[c]))
                if c > 0:
                    dve.wait_ge(maxed[c - 1], g + 2)
                dst = gb[1][:, 0, :] if c == 0 else hl[u][:, 1, :]
                if c:
                    dve.wait_ge(S["cat_transposed"], g)
                V.tensor_reduce(dst, gb[c][:, :, :].rearrange("p k c -> p c k"), AX.X, ALU.max).then_inc(maxed[c], 1)

            o = Order(order)
            V.memset(zrow[:, :], 0.0)
            V.memset(ones[:, :], 1.0).then_inc(S["ones_ready"], 1)
            for c in range(len(CHUNKS)):
                dve.sem_inc(maxed[c], 1)
            dve.wait_ge(S["consts_in"], 16 * 3)
            V.tensor_copy(cb[:, :], val[1][:, 0:C_COLS]).then_inc(S["bf16_ready"], 1)
            for m in range(PAIRS):
                u = m % 2
                dve.wait_ge(first_in[m], 16)
                if m >= 2:
                    dve.wait_ge(S["hn_ready"], m - 1)
                dve.wait_ge(order, o.n)
                statistics(o, first_rows(m)[:, 0, :], 0, u)
                statistics(o, first_rows(m)[:, 1, :], 1, u, S["stats_ready"])
                if m >= 1:
                    normaliser(o, m - 1, 1 - u, slice(0, 2))
                if m == 2:
                    read_words(o, 0)
                    search(o, 0, 0, True, False)
                    search(o, 0, 0, False, True)
            normaliser(o, PAIRS - 1, 1, slice(0, 2))
            dve.wait_ge(S["weights_in"], 16 * 4)
            for k in range(2):
                n = o.mark(V.tensor_tensor(lk[0][:, 0:2 * C].rearrange("p (a o) -> p a o", a=2),
                                           w1[:, k, 0:C].unsqueeze(1).to_broadcast([P, 2, C]),
                                           val[0][:, 0:2 * C].rearrange("p (a o) -> p a o", a=2), ALU.mult))
                dve.wait_ge(order, n)
                n = o.mark(V.tensor_reduce(m_t[:, 0:2], lk[0][:, 0:2 * C].rearrange("p (a o) -> p a o", a=2), AX.X, ALU.add))
                dve.wait_ge(order, n)
                o.mark(V.tensor_copy(w1[:, k, C:C + 1], m_t[:, 1:2]))
                n = o.mark(V.tensor_copy(wa1[:, k, :], m_t[:, 0:1].to_broadcast([P, P])))
                dve.wait_ge(order, n)
            V.engine_nop().then_inc(S["weights_ready"], 1)
            read_words(o, 1)
            search(o, 1, 0, True, False)
            read_words(o, 2)
            search(o, 2, 1, True, True)
            chunk_max(o, 0, 0)
            end_order(o)

            def item_value(o, i, j, jj, sweep, drain):
                off = blocked_of(jj, drain)
                if not (type(i) is int and i < 2):
                    wait_apart(dve, "dve_passed", S["leaky_ready"], i - 1)
                wait_apart(dve, "dve_passed", S["blocked_ready"], i + 1)
                if sweep:
                    V.tensor_tensor(val[jj][:, 0:HALF], off[:, HALF:N], s1_all[:, HALF:N], ALU.add
                                    ).then_inc(S["val_ready"], 1)
                    return
                dve.wait_ge(order, o.n)
                V.tensor_tensor_reduce(out=val[jj][:, :], in0=off[:, :], in1=s1_all[:, :], scale=1.0, scalar=-3e38,
                                       op0=ALU.add, op1=ALU.max, accum_out=m_t[:, jj:jj + 1]
                                       ).then_inc(S["val_ready"], 1)

            def item_bounds(o, i, j):
                dve.wait_ge(S["val_ready"], i + 2)
                o.mark(V.tensor_scalar(m_a[:, 1, :], m_t[:, :], -SLOPE, None, ALU.mult))
                n = o.mark(V.scalar_tensor_tensor(out=m_a[:, 0, :], in0=m_t[:, :], scalar=SLOPE - 1,
                                                  in1=s2n[:, bass.ds(j, 2)], op0=ALU.mult, op1=ALU.add))
                dve.wait_ge(order, n)
                o.mark(V.scalar_tensor_tensor(out=nb[:, bass.ds(j, 2)], in0=m_a[:, 0, :], scalar=0.0,
                                              in1=m_a[:, 1, :], op0=ALU.min, op1=ALU.add))

            def item_leaky(o, i, jj, sweep, u, drain):
                w, q = HALF if sweep else N, lk_of(jj, u, drain)
                dve.wait_ge(S["relu_ready"], i + 1)
                V.scalar_tensor_tensor(out=q[:, 0:w], in0=val[jj][:, 0:w], scalar=SLOPE, in1=q[:, 0:w],
                                       op0=ALU.mult, op1=ALU.add).then_inc(S["leaky_ready"], 1)

            def item_rows(o, i, j, jj, sweep):
                if sweep == 0:
                    dve.wait_ge(S["exp_ready"], i + 1)
                    n = o.mark(V.reciprocal(rz[:, bass.ds(j, 1)], za[:, bass.ds(j, 1)]))
                    dve.wait_ge(order, n)
                dve.wait_ge(S["av_done"], i)
                V.tensor_scalar(hz[jj][:, :], h_all[:, bass.ds(j, 1), 0:C].rearrange("p a c -> p (a c)"),
                                rz[:, bass.ds(j, 1)], None, ALU.mult).then_inc(S["hz_ready"], 1)

            def flush(o, f):
                dve.wait_ge(S["gelu_done"], f + 1)
                dve.wait_ge(S["xo_in"], f * 16 + 16)
                dve.wait_ge(order, o.n)
                V.tensor_tensor(go[:, :, :], go[:, :, :], xo[:, :, :], ALU.add).then_inc(S["res_ready"], 1)

            def take_s1(o, b):
                dve.wait_ge(S["h_saved"], b * TILES)
                if not (type(b) is int and b == 1):
                    dve.wait_ge(S["val_ready"], (b - 1) * 32)
                o.mark(V.tensor_copy(s1_all[:, :], s1_acc[:, :]))

            def take_s2(o, b):
                o.mark(V.tensor_scalar(s2p[:, :], h_acc[:, :, C], 1 - SLOPE, None, ALU.mult))
                V.tensor_scalar(s2n[:, :], h_acc[:, :, C], SLOPE - 1, None, ALU.mult).then_inc(S["s_copied"], 1)

            def step(o, b, i, u, t, n, words, nodes, l, g, new, old, fl, drain):
                v = b * TILES + i * 2 + u
                it = (b - 1) * 32 + i * 4 + u * 2
                sweep, before = t // 8 % 2, (t - 1) // 8 % 2
                j = i * 4 + u * 2 - 16 * sweep
                j1 = j - 1 if t % 8 else 15
                j2 = j - 2 if t % 8 else 14
                if l:
                    chunk_max(o, 1, v, u)
                if new:
                    if not t:
                        take_s1(o, b)
                    item_value(o, it, j, 0, sweep, drain)
                if old and drain:
                    item_leaky(o, it - 1, 1, before, 1 - u, drain)
                if old:
                    if t == 1:
                        wait_apart(dve, "dve_passed", S["h_copied"], b)
                    item_rows(o, it - 2, j2, 0, before)
                    if not t:
                        item_rows(o, it - 1, j1, 1, before)
                if old and not drain:
                    item_leaky(o, it - 1, 1, before, 1 - u, drain)
                if new and not t:
                    take_s2(o, b)
                if words:
                    read_words(o, v + 3)
                if l:
                    if n:
                        m = (b + 1) * PAIRS + i * 2 + u - N_FIRST
                        dve.wait_ge(xn_in[u], b * 64 + (i - N_FIRST // 2) * 16 + 16)
                        dve.wait_ge(S["hn_ready"], m - 1)
                        o.mark(V.bn_stats(bn6[:, 0, :], xn[u][:, 0, :]))
                        n3 = o.mark(V.bn_stats(bn6[:, 1, :], xn[u][:, 1, :]))
                    dve.wait_ge(S["out0_done"], v + 1)
                    dve.wait_ge(l_in[u], (b * PAIRS + i) * 32 + 32)
                    dve.wait_ge(x1_stored[u], (b * PAIRS + i) * 16)
                    n1 = o.mark(V.scalar_tensor_tensor(out=x1[u][:, :], in0=ps_l[:, 0:C], scalar=0.0,
                                                       in1=xl[u][:, :], op0=ALU.max, op1=ALU.add))
                    dve.wait_ge(order, n1)
                    n1 = o.mark(V.bn_stats(bn6[:, 2, :], x1[u][:, :]))
                    if n:
                        dve.wait_ge(order, n3)
                        o.mark(V.bn_aggr(mv[u][:, 0, :], bn6[:, 0, :]))
                        o.mark(V.bn_aggr(mv[u][:, 1, :], bn6[:, 1, :]))
                    dve.wait_ge(order, n1)
                    V.bn_aggr(mv[u][:, 2, :], bn6[:, 2, :]).then_inc(S["stats_ready"], 1)
                if nodes:
                    search(o, v + 3, u, words, nodes)
                if l:
                    normaliser(o, PAIRS + v, u, slice(0 if n else 2, 3))
                if g:
                    chunk_max(o, 0, v + 1)
                if fl is not None:
                    flush(o, fl)
                if new:
                    item_value(o, it + 1, j + 1, 1, sweep, drain)
                if new and sweep == 0:
                    if not t:
                        wait_apart(dve, "dve_passed", S["s_copied"], b)
                    item_bounds(o, it, j)
                if new and drain:
                    item_leaky(o, it, 0, sweep, u, drain)
                if old and t:
                    item_rows(o, it - 1, j1, 1, before)
                if new and not drain:
                    item_leaky(o, it, 0, sweep, u, drain)

            def round_(b, first=False, last=False, drain=False):
                def pair(i, t0):
                    o = Order(order)
                    for u in range(2):
                        t = t0 + u
                        one = type(b) is int and b == 1
                        fl = {1: b * 2 - 3, 9: b * 2 - 2}.get(t) if not first and not (one and t == 1) else None
                        step(o, b, i, u, t, n=0 <= t - N_FIRST < PAIRS and not last and not drain,
                             words=not drain and not (last and t >= 13), nodes=not drain and not (last and t >= 14),
                             l=not drain, g=not drain and not (last and t == 15),
                             new=not first, old=not first and not (one and t == 0), fl=fl, drain=drain)
                    end_order(o)
                for t0, i0, end in SECTIONS[last]:
                    if end == i0 + 1:
                        pair(i0, t0)
                    else:
                        with dve.Fori(i0, end) as i:
                            pair(i, t0)

            round_(0, first=True)
            round_(1)
            with dve.Fori(2, NB - 1) as b:
                round_(b)
            round_(NB - 1, last=True)
            round_(NB, drain=True)
            o = Order(order)
            step(o, NB + 1, 0, 0, 0, n=False, words=False, nodes=False, l=False, g=False, new=False, old=True,
                 fl=None, drain=True)
            flush(o, 2 * NB - 1)

        @block.tensor
        def _(pe):
            T = nc.tensor

            def transpose_signs(a):
                pe.wait_ge(S["signed"], a + 1)
                pe.wait_ge(S["edges_ready"], a)
                pe.wait_ge(S["words_read"], a)
                for m in range(TILES):
                    ins = T.transpose(sgt[:, m * P:(m + 1) * P], sg[:, m * P:(m + 1) * P], identb)
                ins.then_inc(S["signs_transposed"], 1)

            def make_words(a):
                pe.wait_ge(S["bits_ready"], a + 1)
                pe.wait_ge(S["edges_ready"], a + 1)
                for m in range(TILES):
                    T.matmul(words[:, m * 16:(m + 1) * 16], bits[:, m, :], pack, start=True, stop=True)
                T.matmul(keyed, one_row, key_row, start=True, stop=False)
                for m in range(TILES):
                    ins = T.matmul(keyed[:, m * 16:(m + 1) * 16], bits[:, m, :], pack, start=False, stop=m == TILES - 1)
                ins.then_inc(S["words_done"], 1)

            def av(i, jj, u, drain):
                pe.wait_ge(S["exp_ready"], i + 1)
                pe.wait_ge(S["hz_ready"], i + 1)
                for k in range(8):
                    ins = T.matmul(ps_av[:, k * C:(k + 1) * C], lk_of(jj, u, drain)[:, k * P:(k + 1) * P], hz[jj][:, :],
                                   start=False, stop=False)
                ins.then_inc(S["av_done"], 1)

            def open_sweep(f):
                if not (type(f) is int and f == 0):
                    pe.wait_ge(S["gelu_done"], f)
                for k in range(4):
                    T.matmul(ps_av[:, k * 512:(k + 1) * 512], zeros[0:1, 0:P], zeros[0:1, :], start=True, stop=False)

            def close_sweep():
                for k in range(4):
                    ins = T.matmul(ps_av[:, k * 512:(k + 1) * 512], zeros[0:1, 0:P], zeros[0:1, :], start=False, stop=True)
                ins.then_inc(S["sweep_done"], 1)

            def step(b, i, u, t, a, l, old, drain):
                v = b * TILES + i * 2 + u
                it = (b - 1) * 32 + i * 4 + u * 2
                if l:
                    pe.wait_ge(l_in[u], (b * PAIRS + i) * 32 + 32)
                    pe.wait_ge(maxed[1], v + 2)
                    for k in range(4):
                        ins = T.transpose(ps_t[:, k * P:(k + 1) * P], hl[u][:, k // 2, k % 2 * P:(k % 2 + 1) * P], ident)
                    ins.then_inc(S["cat_transposed"], 1)
                    pe.wait_ge(S["cat_ready"], v + 1)
                    pe.wait_ge(S["h_saved"], v)
                    for k in range(4):
                        T.matmul(ps_l[:, 0:C], hcat[:, k, :], w0[:, k, :], start=k == 0, stop=False)
                    T.matmul(ps_l[:, 0:C], ones[:, :], bias0[:, :], start=False, stop=True).then_inc(S["out0_done"], 1)
                if old and t % 8 == 1:
                    open_sweep(b * 2 - 2 + t // 8)
                if old:
                    av(it - 2, 0, 1 - u, drain)
                if a:
                    transpose_signs(v + 4)
                if l:
                    pe.wait_ge(S["y1_ready"], v + 1)
                    for k in range(2):
                        ins = T.transpose(ps_t[:, k * P:(k + 1) * P], y1[:, k * P:(k + 1) * P], ident)
                    ins.then_inc(S["y1_transposed"], 1)
                if a:
                    make_words(v + 4)
                if l:
                    pe.wait_ge(S["h1t_ready"], v + 1)
                    for k in range(2):
                        T.matmul(ps_l[:, 0:C + 1], h1t[:, k, :], w1[:, k, :], start=k == 0, stop=k == 1)
                    for k in range(2):
                        ins = T.matmul(ps_l[:, 384:384 + P], wa1[:, k, :], h1t[:, k, :], start=k == 0, stop=k == 1)
                    ins.then_inc(S["h_done"], 1)
                if old:
                    av(it - 1, 1, 1 - u, drain)
                    if t % 8 == 0:
                        close_sweep()

            pe.sem_inc(S["av_done"], 1)
            pe.wait_ge(S["bf16_ready"], 1)
            pe.wait_ge(S["ones_ready"], 1)
            pe.wait_ge(S["zeros_ready"], 1)
            for a in range(4):
                transpose_signs(a)
                make_words(a)
            pe.wait_ge(S["consts_in"], 16 * 3)
            pe.wait_ge(S["weights_in"], 16 * 4)
            pe.wait_ge(S["weights_ready"], 1)

            def round_(b, first=False, last=False, drain=False):
                def pair(i, t0):
                    for u in range(2):
                        t = t0 + u
                        step(b, i, u, t, a=not drain and not (last and t >= 12), l=not drain,
                             old=not first and not (type(b) is int and b == 1 and t == 0), drain=drain)
                for t0, i0, end in SECTIONS[last]:
                    if end == i0 + 1:
                        pair(i0, t0)
                    else:
                        with pe.Fori(i0, end) as i:
                            pair(i, t0)

            round_(0, first=True)
            round_(1)
            with pe.Fori(2, NB - 1) as b:
                round_(b)
            round_(NB - 1, last=True)
            round_(NB, drain=True)
            step(NB + 1, 0, 0, 0, a=False, l=False, old=True, drain=True)


def constants():
    import numpy as np
    f = np.zeros((P, C_COLS), np.float32)
    f[:, C_ID:C_ID + P] = np.eye(P)
    f[:, C_ONE:C_ONE + P] = 1.0
    f[:, C_KEY:C_KEY + WORDS] = (WORDS - np.arange(WORDS)) * (1 << WORD)
    f[:, C_IOTA:C_IOTA + WORD] = np.arange(WORD)
    for m in range(P):
        f[m, C_PACK + m // WORD] = 2.0 ** (WORD - 1 - m % WORD)
    i = np.zeros((P, WORD), np.int32)
    i[:, :] = 1 << (WORD - 1 - np.arange(WORD))
    return {"const_f": f, "const_i": i}


def kernel(x, adj, L0_gnn_W, L0_gnn_b, L1_gnn_W, L1_gnn_a):
    import numpy as np
    import concourse.bacc as bacc
    from concourse.bass_utils import run_bass_kernel_spmd

    nc = bacc.Bacc("TRN2", target_bir_lowering=False, num_devices=1)
    given = {"x": x, "adj": adj, "L0_gnn_W": L0_gnn_W, "L0_gnn_b": L0_gnn_b, "L1_gnn_W": L1_gnn_W,
             "L1_gnn_a": L1_gnn_a, **constants()}
    arrays = {f"in_{k}": np.ascontiguousarray(v) for k, v in given.items()}
    args = [nc.dram_tensor(k, a.shape, mybir.dt.from_np(a.dtype), kind="ExternalInput").ap() for k, a in arrays.items()]
    out = nc.dram_tensor("out_0", (NB, N, C), fp32, kind="ExternalOutput").ap()
    graph_layers(nc, *args, out)
    return run_bass_kernel_spmd(nc, [arrays], core_ids=[0]).results[0]["out_0"]
```
